# Optimizing a Trainium2 kernel written in Bass

```python
import numpy as np
import jax
import jax.numpy as jnp

def _softmax(x, axis=-1):
    return jax.nn.softmax(x, axis=axis)

def _gelu(x):
    return jax.nn.gelu(x, approximate=True)

def _silu(x):
    return jax.nn.silu(x)

def _sigmoid(x):
    return jax.nn.sigmoid(x)

def _layernorm(x, axis=-1, eps=1e-05):
    m = jnp.mean(x, axis=axis, keepdims=True)
    v = jnp.var(x, axis=axis, keepdims=True)
    return (x - m) / jnp.sqrt(v + eps)

def _scatter_add(tgt, idx, src, axis=0):
    return tgt.at[idx].add(src)

def _segment_sum(src, seg, n):
    return jax.ops.segment_sum(src, seg, n)
kernel_name = 'mk_seq_postln_d2_jaxref_r8_3fba18'

def setup_inputs(seed: int=0):
    np.random.seed(seed)
    _w = jnp.asarray

    def _L0_attn_setup():
        import jax, jax.numpy as jnp
        import numpy as np
        B, T, C = (8, 256, 128)
        HS = 64
        H = C // HS
        LORA_R = 32
        TD_R = 64

        def _wkv6(r, k, v, w, u):
            n = r.shape[-1]
            decay = jnp.exp(-jnp.exp(w))

            def per_head(rt, kt, vt, dt, uh):

                def step(S, inp):
                    ri, ki, vi, di = inp
                    kv = ki[:, None] * vi[None, :]
                    y = ri @ (S + uh[:, None] * kv)
                    S = di[:, None] * S + kv
                    return (S, y)
                S0 = jnp.zeros((n, n), rt.dtype)
                _, ys = jax.lax.scan(step, S0, (rt, kt, vt, dt))
                return ys
            f = jax.vmap(per_head, in_axes=(0, 0, 0, 0, 0))
            f = jax.vmap(f, in_axes=(0, 0, 0, 0, None))
            return f(r, k, v, decay, u)
        key = jax.random.key(seed)
        ks = jax.random.split(key, 20)
        inp = {'x': jax.random.normal(ks[0], (B, T, C), jnp.float32), 'miu_x': jax.random.uniform(ks[1], (1, 1, C), jnp.float32), 'lambda_': jax.random.uniform(ks[2], (5, 1, 1, C), jnp.float32), 'A_lora': jax.random.normal(ks[3], (C, LORA_R * 5), jnp.float32) * 0.01, 'B_lora': jax.random.normal(ks[4], (5, LORA_R, C), jnp.float32) * 0.01, 'td_miu': -6.0 + 5.0 * jax.random.uniform(ks[5], (1, 1, C), jnp.float32), 'td_A': jax.random.normal(ks[6], (C, TD_R), jnp.float32) * 0.01, 'td_B': jax.random.normal(ks[7], (TD_R, C), jnp.float32) * 0.01, 'u': jax.random.normal(ks[8], (H, HS), jnp.float32) * 0.1, 'Wr': jax.random.normal(ks[9], (C, C), jnp.float32) * 0.02, 'Wk': jax.random.normal(ks[10], (C, C), jnp.float32) * 0.02, 'Wv': jax.random.normal(ks[11], (C, C), jnp.float32) * 0.02, 'Wg': jax.random.normal(ks[12], (C, C), jnp.float32) * 0.02, 'Wo': jax.random.normal(ks[13], (C, C), jnp.float32) * 0.02, 'gn_gamma': jnp.ones((C,), jnp.float32), 'gn_beta': jnp.zeros((C,), jnp.float32)}
        return inp
    _L0_attn_in = _L0_attn_setup()

    def _L0_ffn_setup():
        import jax, jax.numpy as jnp
        import numpy as np
        B, S, H, DV = (4, 512, 128, 128)
        E, INNER, P, K = (8, 32, 8, 2)

        def _ln(v, g, b, eps=1e-05):
            m = jnp.mean(v, axis=-1, keepdims=True)
            var = jnp.var(v, axis=-1, keepdims=True)
            return (v - m) * jax.lax.rsqrt(var + eps) * g + b
        key = jax.random.key(seed)
        ks = jax.random.split(key, 8)
        sc = lambda d: 1.0 / np.sqrt(d)
        return {'x': jax.random.normal(ks[0], (B, S, H), jnp.float32), 'Wv': jax.random.normal(ks[1], (DV, H), jnp.float32) * sc(H), 'bv': jnp.zeros((DV,), jnp.float32), 'Wg': jax.random.normal(ks[2], (E, DV), jnp.float32) * sc(DV), 'bg': jnp.zeros((E,), jnp.float32), 'Wp': jax.random.normal(ks[3], (E, P, DV), jnp.float32) * sc(DV), 'alpha': jnp.zeros((), jnp.float32), 'g_r': jnp.ones((E,), jnp.float32), 'b_r': jnp.zeros((E,), jnp.float32), 'g_c': jnp.ones((E,), jnp.float32), 'b_c': jnp.zeros((E,), jnp.float32), 'W1': jax.random.normal(ks[4], (E, INNER, DV), jnp.float32) * sc(DV), 'b1': jnp.zeros((E, INNER), jnp.float32), 'W2': jax.random.normal(ks[5], (E, DV, INNER), jnp.float32) * sc(INNER), 'b2': jnp.zeros((E, DV), jnp.float32)}
    _L0_ffn_in = _L0_ffn_setup()

    def _L1_attn_setup():
        import jax, jax.numpy as jnp
        import numpy as np

        def log_g(x):
            return jnp.where(x >= 0, jnp.log(jax.nn.relu(x) + 0.5), -jax.nn.softplus(-x))

        def parallel_scan_log(log_a, log_b):
            log_a_star = jnp.cumsum(log_a, axis=1)
            log_x0_plus_b_star = jax.lax.cumlogsumexp(log_b - log_a_star, axis=1)
            return jnp.exp(log_a_star + log_x0_plus_b_star)
        key = jax.random.key(seed)
        B, T, D = (8, 512, 128)
        k1, k2, k3, k4, k5 = jax.random.split(key, 5)
        scale = 1.0 / np.sqrt(D)
        return {'h_prev_layer': jax.random.normal(k1, (B, T, D), dtype=jnp.float32), 'W_z': jax.random.uniform(k2, (D, D), jnp.float32, -scale, scale), 'b_z': jax.random.uniform(k3, (D,), jnp.float32, -scale, scale), 'W_h': jax.random.uniform(k4, (D, D), jnp.float32, -scale, scale), 'b_h': jax.random.uniform(k5, (D,), jnp.float32, -scale, scale)}
    _L1_attn_in = _L1_attn_setup()

    def _L1_ffn_setup():
        import jax, jax.numpy as jnp
        import numpy as np
        E = 8
        K = 2
        CAP_FACTOR = 1.0
        key = jax.random.key(seed)
        ks = jax.random.split(key, 5)
        B, T, C, H = (4, 256, 128, 512)
        x = jax.random.normal(ks[0], (B, T, C), dtype=jnp.float32)
        Wr = jax.random.normal(ks[1], (C, E), dtype=jnp.float32) * 0.02
        br = jnp.zeros((E,), jnp.float32)
        W1 = jax.random.normal(ks[2], (E, C, H), dtype=jnp.float32) * 0.02
        b1 = jnp.zeros((E, H), jnp.float32)
        W2 = jax.random.normal(ks[3], (E, H, C), dtype=jnp.float32) * 0.02
        b2 = jnp.zeros((E, C), jnp.float32)
        return {'x': x, 'Wr': Wr, 'br': br, 'W1': W1, 'b1': b1, 'W2': W2, 'b2': b2}
    _L1_ffn_in = _L1_ffn_setup()
    _d = {'L0_attn_x': _L0_attn_in['x'], 'L0_attn_miu_x': _L0_attn_in['miu_x'], 'L0_attn_lambda_': _L0_attn_in['lambda_'], 'L0_attn_A_lora': _L0_attn_in['A_lora'], 'L0_attn_B_lora': _L0_attn_in['B_lora'], 'L0_attn_td_miu': _L0_attn_in['td_miu'], 'L0_attn_td_A': _L0_attn_in['td_A'], 'L0_attn_td_B': _L0_attn_in['td_B'], 'L0_attn_u': _L0_attn_in['u'], 'L0_attn_Wr': _L0_attn_in['Wr'], 'L0_attn_Wk': _L0_attn_in['Wk'], 'L0_attn_Wv': _L0_attn_in['Wv'], 'L0_attn_Wg': _L0_attn_in['Wg'], 'L0_attn_Wo': _L0_attn_in['Wo'], 'L0_attn_gn_gamma': _L0_attn_in['gn_gamma'], 'L0_attn_gn_beta': _L0_attn_in['gn_beta'], 'L0_ffn_Wv': _L0_ffn_in['Wv'], 'L0_ffn_bv': _L0_ffn_in['bv'], 'L0_ffn_Wg': _L0_ffn_in['Wg'], 'L0_ffn_bg': _L0_ffn_in['bg'], 'L0_ffn_Wp': _L0_ffn_in['Wp'], 'L0_ffn_alpha': _L0_ffn_in['alpha'], 'L0_ffn_g_r': _L0_ffn_in['g_r'], 'L0_ffn_b_r': _L0_ffn_in['b_r'], 'L0_ffn_g_c': _L0_ffn_in['g_c'], 'L0_ffn_b_c': _L0_ffn_in['b_c'], 'L0_ffn_W1': _L0_ffn_in['W1'], 'L0_ffn_b1': _L0_ffn_in['b1'], 'L0_ffn_W2': _L0_ffn_in['W2'], 'L0_ffn_b2': _L0_ffn_in['b2'], 'L1_attn_W_z': _L1_attn_in['W_z'], 'L1_attn_b_z': _L1_attn_in['b_z'], 'L1_attn_W_h': _L1_attn_in['W_h'], 'L1_attn_b_h': _L1_attn_in['b_h'], 'L1_ffn_Wr': _L1_ffn_in['Wr'], 'L1_ffn_br': _L1_ffn_in['br'], 'L1_ffn_W1': _L1_ffn_in['W1'], 'L1_ffn_b1': _L1_ffn_in['b1'], 'L1_ffn_W2': _L1_ffn_in['W2'], 'L1_ffn_b2': _L1_ffn_in['b2']}
    _x0 = _d['L0_attn_x']
    _d['L0_attn_x'] = jax.random.normal(jax.random.fold_in(jax.random.key(seed), 1), (16, 512, 128), dtype=_x0.dtype)
    del _x0
    return _d

def reference(L0_attn_x, L0_attn_miu_x, L0_attn_lambda_, L0_attn_A_lora, L0_attn_B_lora, L0_attn_td_miu, L0_attn_td_A, L0_attn_td_B, L0_attn_u, L0_attn_Wr, L0_attn_Wk, L0_attn_Wv, L0_attn_Wg, L0_attn_Wo, L0_attn_gn_gamma, L0_attn_gn_beta, L0_ffn_Wv, L0_ffn_bv, L0_ffn_Wg, L0_ffn_bg, L0_ffn_Wp, L0_ffn_alpha, L0_ffn_g_r, L0_ffn_b_r, L0_ffn_g_c, L0_ffn_b_c, L0_ffn_W1, L0_ffn_b1, L0_ffn_W2, L0_ffn_b2, L1_attn_W_z, L1_attn_b_z, L1_attn_W_h, L1_attn_b_h, L1_ffn_Wr, L1_ffn_br, L1_ffn_W1, L1_ffn_b1, L1_ffn_W2, L1_ffn_b2):

    def _L0_attn_ref(x, miu_x, lambda_, A_lora, B_lora, td_miu, td_A, td_B, u, Wr, Wk, Wv, Wg, Wo, gn_gamma, gn_beta):
        import jax, jax.numpy as jnp
        import numpy as np
        B, T, C = (8, 256, 128)
        HS = 64
        H = C // HS
        LORA_R = 32
        TD_R = 64

        def _wkv6(r, k, v, w, u):
            n = r.shape[-1]
            decay = jnp.exp(-jnp.exp(w))

            def per_head(rt, kt, vt, dt, uh):

                def step(S, inp):
                    ri, ki, vi, di = inp
                    kv = ki[:, None] * vi[None, :]
                    y = ri @ (S + uh[:, None] * kv)
                    S = di[:, None] * S + kv
                    return (S, y)
                S0 = jnp.zeros((n, n), rt.dtype)
                _, ys = jax.lax.scan(step, S0, (rt, kt, vt, dt))
                return ys
            f = jax.vmap(per_head, in_axes=(0, 0, 0, 0, 0))
            f = jax.vmap(f, in_axes=(0, 0, 0, 0, None))
            return f(r, k, v, decay, u)
        b, t, c = x.shape
        h, n = u.shape
        x_last = jnp.pad(x, ((0, 0), (1, 0), (0, 0)))[:, :t]
        dxa = x_last - x
        xm = x + dxa * miu_x
        lora_h = jnp.tanh(xm @ A_lora).reshape(b, t, 5, -1)
        miu = lambda_ + jnp.einsum('btfi,fic->fbtc', lora_h, B_lora)
        xx = x[None] + dxa[None] * miu
        w_in, k_in, v_in, r_in, g_in = xx
        k = k_in @ Wk.T
        v = v_in @ Wv.T
        r = r_in @ Wr.T
        g = jax.nn.silu(g_in @ Wg.T)
        w = td_miu + jnp.tanh(w_in @ td_A) @ td_B

        def to_heads(z):
            return z.reshape(b, t, h, n).transpose(0, 2, 1, 3)
        y = _wkv6(to_heads(r), to_heads(k), to_heads(v), to_heads(w), u)
        y = y.transpose(0, 2, 1, 3)
        eps = 1e-05 * h
        mean = y.mean(-1, keepdims=True)
        var = y.var(-1, keepdims=True)
        yn = (y - mean) * jax.lax.rsqrt(var + eps)
        yn = yn * gn_gamma.reshape(h, n) + gn_beta.reshape(h, n)
        yn = yn.reshape(b, t, c)
        return yn * g @ Wo.T

    def _L0_ffn_ref(x, Wv, bv, Wg, bg, Wp, alpha, g_r, b_r, g_c, b_c, W1, b1, W2, b2):
        import jax, jax.numpy as jnp
        import numpy as np
        B, S, H, DV = (4, 512, 128, 128)
        E, INNER, P, K = (8, 32, 8, 2)

        def _ln(v, g, b, eps=1e-05):
            m = jnp.mean(v, axis=-1, keepdims=True)
            var = jnp.var(v, axis=-1, keepdims=True)
            return (v - m) * jax.lax.rsqrt(var + eps) * g + b
        V = jnp.einsum('bsh,dh->bsd', x, Wv) + bv
        Vf = V.reshape(-1, DV)
        r = Vf @ Wg.T + bg
        pv = jnp.einsum('epd,nd->nep', Wp, Vf)
        c = jnp.sqrt(jnp.sum(pv * pv, axis=-1)) / np.sqrt(P)
        s = _ln(r, g_r, b_r) + jax.nn.sigmoid(alpha) * _ln(c, g_c, b_c)
        topv, sel = jax.lax.top_k(s, K)
        w = jax.nn.softmax(topv, axis=-1)
        delta = jnp.zeros_like(Vf)
        for e in range(E):
            h = jax.nn.silu(Vf @ W1[e].T + b1[e])
            out = h @ W2[e].T + b2[e]
            we = jnp.sum(jnp.where(sel == e, w, 0.0), axis=-1)
            delta = delta + out * we[:, None]
        return (Vf + delta).reshape(V.shape)

    def _L1_attn_ref(h_prev_layer, W_z, b_z, W_h, b_h):
        import jax, jax.numpy as jnp
        import numpy as np

        def log_g(x):
            return jnp.where(x >= 0, jnp.log(jax.nn.relu(x) + 0.5), -jax.nn.softplus(-x))

        def parallel_scan_log(log_a, log_b):
            log_a_star = jnp.cumsum(log_a, axis=1)
            log_x0_plus_b_star = jax.lax.cumlogsumexp(log_b - log_a_star, axis=1)
            return jnp.exp(log_a_star + log_x0_plus_b_star)
        k = jnp.einsum('btd,ed->bte', h_prev_layer, W_z) + b_z
        tilde_h = jnp.einsum('btd,ed->bte', h_prev_layer, W_h) + b_h
        log_z = -jax.nn.softplus(-k)
        log_one_minus_z = -jax.nn.softplus(k)
        log_tilde_h = log_g(tilde_h)
        return parallel_scan_log(log_one_minus_z, log_z + log_tilde_h)

    def _L1_ffn_ref(x, Wr, br, W1, b1, W2, b2):
        import jax, jax.numpy as jnp
        import numpy as np
        E = 8
        K = 2
        CAP_FACTOR = 1.0
        B, T, C = x.shape
        N = B * T
        xf = x.reshape(N, C)
        logits = xf @ Wr + br
        topv, topi = jax.lax.top_k(logits, K)
        gates = jax.nn.softmax(topv, axis=-1)
        rw = jnp.zeros((N, E), xf.dtype).at[jnp.arange(N)[:, None], topi].set(gates)
        cap = int(N * K / E * CAP_FACTOR)
        sel = jax.nn.one_hot(topi, E, dtype=jnp.int32).sum(1)
        rank = jnp.cumsum(sel, axis=0) - sel
        keep = (sel > 0) & (rank < cap)
        tok = jnp.broadcast_to(jnp.arange(N, dtype=jnp.int32)[:, None], (N, E))
        eid = jnp.broadcast_to(jnp.arange(E, dtype=jnp.int32)[None, :], (N, E))
        rank_c = jnp.where(keep, rank, cap)
        buf = jnp.full((E, cap), N, dtype=jnp.int32)
        buf = buf.at[eid, rank_c].set(tok, mode='drop')
        xpad = jnp.concatenate([xf, jnp.zeros((1, C), xf.dtype)], axis=0)
        xg = xpad[buf]
        h = jax.nn.gelu(jnp.einsum('ecd,edh->ech', xg, W1) + b1[:, None, :], approximate=False)
        out = jnp.einsum('ech,ehd->ecd', h, W2) + b2[:, None, :]
        rw_pad = jnp.concatenate([rw, jnp.zeros((1, E), rw.dtype)], axis=0)
        w = rw_pad[buf, jnp.arange(E, dtype=jnp.int32)[:, None]]
        weighted = out * w[..., None]
        final = jnp.zeros((N + 1, C), xf.dtype).at[buf.reshape(-1)].add(weighted.reshape(-1, C))
        return final[:N].reshape(B, T, C)
    x = L0_attn_x
    x = _layernorm(x + _L0_attn_ref(x, L0_attn_miu_x, L0_attn_lambda_, L0_attn_A_lora, L0_attn_B_lora, L0_attn_td_miu, L0_attn_td_A, L0_attn_td_B, L0_attn_u, L0_attn_Wr, L0_attn_Wk, L0_attn_Wv, L0_attn_Wg, L0_attn_Wo, L0_attn_gn_gamma, L0_attn_gn_beta), axis=-1)
    x = _layernorm(x + _L0_ffn_ref(x, L0_ffn_Wv, L0_ffn_bv, L0_ffn_Wg, L0_ffn_bg, L0_ffn_Wp, L0_ffn_alpha, L0_ffn_g_r, L0_ffn_b_r, L0_ffn_g_c, L0_ffn_b_c, L0_ffn_W1, L0_ffn_b1, L0_ffn_W2, L0_ffn_b2), axis=-1)
    x = _layernorm(x + _L1_attn_ref(x, L1_attn_W_z, L1_attn_b_z, L1_attn_W_h, L1_attn_b_h), axis=-1)
    x = _layernorm(x + _L1_ffn_ref(x, L1_ffn_Wr, L1_ffn_br, L1_ffn_W1, L1_ffn_b1, L1_ffn_W2, L1_ffn_b2), axis=-1)
    return x

_drawn_inputs = setup_inputs


def setup_inputs(seed=0):
    import zlib

    import numpy as np

    out = dict(_drawn_inputs(seed))
    spreads = {'L0_attn_gn_gamma': (1.0, 0.6),
     'L0_attn_gn_beta': (0.0, 0.587),
     'L0_ffn_bv': (0.0, 0.1),
     'L0_ffn_bg': (0.0, 0.1),
     'L0_ffn_g_r': (1.0, 0.2),
     'L0_ffn_b_r': (0.0, 0.1),
     'L0_ffn_g_c': (1.0, 0.2),
     'L0_ffn_b_c': (0.0, 0.1),
     'L0_ffn_b1': (0.0, 0.1),
     'L0_ffn_b2': (0.0, 0.1),
     'L1_ffn_br': (0.0, 0.1),
     'L1_ffn_b1': (0.0, 0.491),
     'L1_ffn_b2': (0.0, 0.1)}
    factors = {'L0_attn_miu_x': 8.0,
     'L0_attn_A_lora': 8.0,
     'L0_attn_B_lora': 8.0,
     'L0_attn_td_A': 44.355,
     'L0_attn_td_B': 49.547,
     'L0_attn_u': 27.129,
     'L1_attn_b_z': 8.0}
    for name, (base, spread) in spreads.items():
        noise = np.random.default_rng([zlib.crc32(name.encode()), seed]).standard_normal(out[name].shape)
        drawn = base * np.exp(spread * noise) if base else spread * noise
        out[name] = jnp.asarray(drawn.astype(out[name].dtype))
    for name, factor in factors.items():
        out[name] = (out[name] * factor).astype(out[name].dtype)
    return out
```

```python
from contextlib import ExitStack

import concourse.bass as bass
from concourse import mybir

ALU = mybir.AluOpType
ACT = mybir.ActivationFunctionType
F32 = mybir.dt.float32
U32 = mybir.dt.uint32
AX_X = mybir.AxisListType.X

P = 128
T = 512
B = 16
SUB = T // P
HEADS, HS = 2, 64
RANK = 32
MIXES = 5
TD = 64
E0, INNER, PROTO = 8, 32, 8
E1, HID = 8, 512
CAP = B * T * 2 // E1
SLOTS = E1 * CAP
LEVELS = 6
TILE = 512
EPS = 1e-5
BIG = 1.0e30

FIELDS = [
    ("ident", P), ("centre", P), ("group_centre", P), ("upper", P), ("ones", P), ("mean_col", 2),
    ("group_var", HEADS), ("spread", 2 * P), ("descend", SUB * E0), ("slot_base", SUB * E1),
    ("lora_a", RANK * MIXES), ("lora_b", P), ("lora_b4", P), ("td_a", TD), ("td_b", P),
    ("wk", P), ("wv", P), ("wr", P), ("wg", P), ("wo", P),
    ("fv", P), ("fv_raw", P), ("f_router", E0 * (1 + PROTO)), ("f_w1", 2 * P), ("f_w2", 2 * P), ("f_b2", E0),
    ("wz", P), ("wh", P), ("e_router", E1),
    ("miu_x", 1), ("lam", MIXES), ("td_miu", 1), ("bonus", 1), ("gn_gamma", 1), ("gn_beta", 1),
    ("f_bv", 1), ("f_b1", 2), ("b_z", 1), ("b_h", 1),
    ("f_bg", E0), ("f_gr", E0), ("f_br", E0), ("f_gc", E0), ("f_bc", E0), ("alpha", 1), ("e_br", E1),
]
WIDTH = sum(w for _, w in FIELDS)
KT = HID // P
EXPERT_WIDTH = 2 * HID + KT + P


def build_network(nc, x_t, params, masks, experts, out):
    with ExitStack() as ctx:
        def sb(name, shape, dt=F32):
            return ctx.enter_context(nc.sbuf_tensor(name, shape, dt))

        def sems(text):
            return {n: ctx.enter_context(nc.semaphore(n)) for n in text.split()}

        slots_in = nc.dram_tensor("slots_in", [SLOTS, P], F32, kind="Internal").ap()
        slots_out = nc.dram_tensor("slots_out", [SLOTS, P], F32, kind="Internal").ap()
        rows = nc.dram_tensor("rows_after_gru", [B, P, SUB, P], F32, kind="Internal").ap()

        par = sb("par", [P, WIDTH])
        col, at = {}, 0
        for name, w in FIELDS:
            col[name] = (at, w)
            at += w

        def p(name, lo=0, hi=None, parts=P):
            start, w = col[name]
            return par[0:parts, start + lo:start + (w if hi is None else hi)]

        mask = sb("mask", [P, LEVELS + 1, 64], U32)
        folded = sb("folded", [P, 5 * P])
        c_wo, c_fv = folded[:, 0:P], folded[:, P:2 * P]
        c_w2 = [folded[:, (2 + n) * P:(3 + n) * P] for n in range(2)]
        c_quarter = folded[:, 4 * P:5 * P]
        c_b2 = sb("c_b2", [E0, P])
        small = sb("small", [P, 64])
        half_beta, c_bv = small[:, 0:1], small[:, 1:2]
        half_b1, half_bz, half_bh, double_bh = small[:, 2:4], small[:, 4:5], small[:, 5:6], small[:, 6:7]
        sig_alpha = small[:, 7:8]
        router_scale = sb("router_scale", [P, 2, E0])
        router_shift = sb("router_shift", [P, E0])
        powers = sb("powers", [P, 2, 64])
        zeros = sb("zeros", [P, 16 * P])

        x_in = sb("x_in", [P, T + 1])
        dx = sb("dx", [P, T])
        x_mixed = sb("x_mixed", [P, T])
        lora = sb("lora", [P, T])
        lora4 = sb("lora4", [RANK, T])
        mixed = sb("mixed", [P, MIXES, T])
        td_hid = sb("td_hid", [TD, T])
        exp_w = sb("exp_w", [P, T])
        tanh_g = sb("tanh_g", [P, T])
        key = sb("key", [P, T])
        recep = sb("recep", [P, T])
        recep_u = sb("recep_u", [P, T])
        decay = sb("decay", [P, T])
        value = sb("value", [P, SUB, P])
        value_lo = sb("value_lo", [P, SUB, P])
        value_hi = sb("value_hi", [P, SUB, P])
        gate = sb("gate", [P, T])
        total = sb("total", [P, T])
        att = sb("att", [P, HEADS, SUB, 64])
        att_off = sb("att_off", [P, HEADS, SUB, 64])
        key_rows = sb("key_rows", [P, SUB - 1, P])
        state = sb("state", [P, SUB - 1, P])
        y_sb = sb("y_sb", [P, T])
        wkv_sq = sb("wkv_sq", [P, T])
        wkv_cen = sb("wkv_cen", [P, T])
        gated = sb("gated", [P, T])
        gn_var, gn_rstd = sb("gn_var", [P, SUB * HEADS]), sb("gn_rstd", [P, SUB * HEADS])
        ln1_var, ln1_rstd = sb("ln1_var", [P, SUB]), sb("ln1_rstd", [P, SUB])
        x_res = sb("x_res", [P, T])
        x1 = sb("x1", [P, T])
        val = sb("val", [P, T])
        proto_sq = sb("proto_sq", [P, SUB, E0 * PROTO])
        rc = sb("rc", [P, 2, SUB, E0])
        rc_sum = sb("rc_sum", [P, 2 * SUB])
        rc_cen = sb("rc_cen", [P, 2, SUB, E0])
        rc_sq = sb("rc_sq", [P, 2, SUB, E0])
        rc_rstd = sb("rc_rstd", [P, 2 * SUB])
        rc_norm = sb("rc_norm", [P, 2, SUB, E0])
        norm_sq = sb("norm_sq", [P, SUB, E0])
        expert_w = sb("expert_w", [P, SUB, E0])
        expert_wt = sb("expert_wt", [E0, T])
        tanh_h = sb("tanh_h", [P, 2, T])
        half_h = sb("half_h", [P, 2, T])
        hid = sb("hid", [P, 2, T])
        ffn_sq = sb("ffn_sq", [P, T])
        ffn_cen = sb("ffn_cen", [P, T])
        ln2_var, ln2_rstd = sb("ln2_var", [P, SUB]), sb("ln2_rstd", [P, SUB])
        x2 = sb("x2", [P, T])
        tanh_z = sb("tanh_z", [P, T])
        tanh_t = sb("tanh_t", [P, T])
        lin_t = sb("lin_t", [P, T])
        keep_z = sb("keep_z", [P, T])
        take_z = sb("take_z", [P, T])
        hidden = sb("hidden", [P, T])
        gru_sq = sb("gru_sq", [P, T])
        gru_cen = sb("gru_cen", [P, T])
        ln3_var, ln3_rstd = sb("ln3_var", [P, SUB]), sb("ln3_rstd", [P, SUB])
        x3 = sb("x3", [P, T])
        x3_rows = sb("x3_rows", [P, SUB, P])
        logits = sb("logits", [P, SUB, E1])
        chosen = sb("chosen", [P, SUB, E1])
        seen = sb("seen", [P, SUB + 1, E1])
        over = sb("over", [P, SUB, E1])
        slot_of = sb("slot_of", [P, SUB, E1])
        pick_tmp = sb("pick_tmp", [P, SUB, 2, E1])
        slot_f = sb("slot_f", [P, SUB, 2])
        slot_scatter = sb("slot_scatter", [P, SUB * 2], U32)
        kept = sb("kept", [P, SUB, 2])
        slot_all = sb("slot_all", [P, B * SUB * 2], U32)
        gate_all = sb("gate_all", [P, B * SUB * 2])

        class Top2:

            def __init__(self, tag):
                self.best = sb(tag + "best", [P, 2, SUB])
                self.equal = sb(tag + "equal", [P, SUB, E0])
                self.rank = sb(tag + "rank", [P, SUB])
                self.hot = sb(tag + "hot", [P, 2, SUB, E0])
                self.rest = sb(tag + "rest", [P, SUB, E0])
                self.gap = sb(tag + "gap", [P, SUB])
                self.ratio = sb(tag + "ratio", [P, SUB])
                self.den = sb(tag + "den", [P, SUB])
                self.share = sb(tag + "share", [P, SUB, 2])

        ffn_top, gru_top = Top2("ffn_"), Top2("gru_")

        bank = {n: ctx.enter_context(nc.psum_tensor(n, [P, T], F32))
                for n in ("mix0", "mix1", "ffn0", "ffn1", "gru0", "gru1")}
        wkv_banks = ctx.enter_context(nc.psum_tensor("wkv_banks", [P, 2 * T], F32))
        wkv0, wkv1 = wkv_banks[:, 0:T], wkv_banks[:, T:2 * T]
        by_head = wkv_banks[:, :].rearrange("p (h n t) -> p h n t", h=HEADS, t=64)[:, :, 0:SUB, :]
        mix0, mix1 = bank["mix0"], bank["mix1"]
        ffn0, ffn1, gru0, gru1 = bank["ffn0"], bank["ffn1"], bank["gru0"], bank["gru1"]

        sem = sems(
            "pe_passed dve_passed pool_passed params_in masks_in zeroed_slots cleared alpha_tanh setup_dve setup_pe setup_done"
            " x_in_loaded dx_ready x_mixed_ready lora_ps lora_ready miu_ps mixed_part mixed_ready"
            " td_ps td_ready w_ps exp_w_ready decay_ready k_ps key_ready r_ps recep_ready v_ps value_ready g_ps tanh_g_ready gate_ready"
            " x_res_loaded level_ps att_copied level_scaled off_ps off_ready key_t_ps key_rows_ready intra_ps"
            " kv_ps state_step state_ready y_ps y_ready gn_cen_ps gn_sq_ready gn_cen_ready gn_var_ps gn_var_ready gn_rstd_ready gn_bc_ps"
            " gated_step gated_ready o_ps ln1_sq_ready ln1_cen_ready ln1_var_ps ln1_var_ready ln1_rstd_ready ln1_bc_ps x1_ready"
            " val_ps val_ready router_ps proto_sq_ready router_step norm_sq_ready norm_ready rc_sq_ready rc_rstd_ready ffn_gap_ready ffn_ratio_ready"
            " expert_w_ready wt_ps wt_ready h_ps h_read silu_ready spread_ps hid_ready delta_ps ln2_sq_ready ln2_cen_ready"
            " ln2_var_ps ln2_var_ready ln2_rstd_ready ln2_bc_ps x2_ready"
            " z_ps t_ps z_read t_read gru_step hidden_ready g_out_ps ln3_sq_ready ln3_cen_ready ln3_var_ps ln3_var_ready ln3_rstd_ready"
            " ln3_bc_ps x3_ready logits_ps rows_ps rows_ready rows_stored route_step gru_gap_ready gru_ratio_ready chosen_ready rank_ps"
            " slots_ready scattered"
            " w_loaded0 w_loaded1 slots_loaded0 slots_loaded1 slot_t_ps slot_t_ready up_ps act_ready down_ps exp_out_ready exp_stored0 exp_stored1"
            " pick_ready gathered0 gathered1 rows_loaded0 rows_loaded1 comb_half comb_ready bn_ready mean_ready last_var_ready"
            " last_rstd_ready y_out_ready out_stored0 out_stored1")

        expert_par = sb("expert_par", [P, 2, EXPERT_WIDTH])

        def w1_of(s, m):
            return expert_par[:, s, m * P:(m + 1) * P]

        def w2_of(s, k):
            return expert_par[:, s, HID + k * P:HID + (k + 1) * P]

        def b1_of(s, m):
            return expert_par[:, s, 2 * HID + m:2 * HID + m + 1]

        def b2_of(s):
            return expert_par[:, s, 2 * HID + KT:2 * HID + KT + P]

        tile_in = sb("tile_in", [P, 2, SUB, P])
        tile_t = sb("tile_t", [P, 2, TILE])
        act_h = sb("act_h", [P, 2, KT, TILE])
        tile_out = sb("tile_out", [P, 2, SUB, P])
        pick = sb("pick", [P, 2, SUB * 2], U32)
        pick_gate = sb("pick_gate", [P, 2, SUB * 2])
        got = sb("got", [P, 2, SUB * 2, P])
        y_rows = sb("y_rows", [P, 2, SUB, P])
        y_out = sb("y_out", [P, 2, SUB, P])
        bn = sb("bn", [P, SUB, 6])
        mean_var = sb("mean_var", [P, 2, SUB, 2])
        last_var, last_rstd = sb("last_var", [P, 2, SUB]), sb("last_rstd", [P, 2, SUB])

        tiles_per = CAP // TILE
        tiles_turn = 2 * tiles_per
        slot_tiles_in = slots_in.rearrange("(g p r) c -> g p r c", p=P, r=SUB)
        slot_tiles_out = slots_out.rearrange("(g p r) c -> g p r c", p=P, r=SUB)
        up_banks, down_banks, turn_banks = (wkv0, wkv1, ffn0, ffn1), (gru0, gru1), (mix0, mix1)
        w_loaded, slots_loaded, exp_stored = (sem["w_loaded0"], sem["w_loaded1"]), (sem["slots_loaded0"], sem["slots_loaded1"]), (sem["exp_stored0"], sem["exp_stored1"])
        gathered, rows_loaded, out_stored = (sem["gathered0"], sem["gathered1"]), (sem["rows_loaded0"], sem["rows_loaded1"]), (sem["out_stored0"], sem["out_stored1"])

        def past(eng, signal, value):
            if not (isinstance(value, int) and value <= 0):
                eng.wait_ge(signal, value)

        def turns(eng, count, turn, peeled=1):
            for n in range(peeled):
                turn(n, n == 0, False)
            with eng.Fori(peeled, count - 1) as n:
                turn(n, False, False)
            turn(count - 1, False, True)

        def experts_sp(sp):
            def weights(e, s):
                sp.dma_start(expert_par[:, s, :], experts[e]).then_inc(w_loaded[s], 16)

            def load(g, b):
                sp.dma_start(tile_in[:, b, :, :], slot_tiles_in[g]).then_inc(slots_loaded[b], 16)

            weights(0, 0)
            weights(1, 1)
            sp.wait_ge(sem["scattered"], 16 * 2 * SUB * B)
            load(0, 0)
            load(1, 1)

            def turn(pair, first, final):
                for u in range(tiles_turn):
                    g = pair * tiles_turn + u
                    if not (final and u >= tiles_turn - 2):
                        sp.wait_ge(sem["slot_t_ps"], g + 1)
                        load(g + 2, u % 2)
                    if u == tiles_per and not final:
                        sp.wait_ge(sem["down_ps"], g)
                        weights(pair * 2 + 2, 0)
                    sp.wait_ge(sem["exp_out_ready"], g + 1)
                    sp.dma_start(slot_tiles_out[g], tile_out[:, u % 2, :, :]).then_inc(exp_stored[u % 2], 16)
                if not final:
                    sp.wait_ge(sem["down_ps"], (pair + 1) * tiles_turn)
                    weights(pair * 2 + 3, 1)

            turns(sp, E1 // 2, turn)

        def experts_pe(pe):
            mm = pe.matmul

            def transpose_tile(g, b):
                past(pe, sem["slot_t_ready"], g - 1)
                pe.wait_ge(slots_loaded[b], (g - b) * 8 + 16)
                for r in range(SUB):
                    last = pe.transpose(turn_banks[b][:, r * P:(r + 1) * P], tile_in[:, b, r, :], p("ident"))
                last.then_inc(sem["slot_t_ps"], 1)

            pe.wait_ge(sem["gate_ready"], B)
            pe.wait_ge(sem["x1_ready"], B)
            pe.wait_ge(sem["x2_ready"], B)
            pe.wait_ge(sem["rows_ready"], B)
            pe.wait_ge(sem["slots_ready"], B)
            transpose_tile(0, 0)

            def turn(pair, first, final):
                for u in range(tiles_turn):
                    g, b, s = pair * tiles_turn + u, u % 2, u // tiles_per
                    if u % tiles_per == 0:
                        pe.wait_ge(w_loaded[s], pair * 16 + 16)
                    pe.wait_ge(sem["slot_t_ready"], g + 1)
                    for m in range(KT):
                        past(pe, sem["act_ready"], (g - 1) * KT + m + 1)
                        mm(up_banks[m][:, :], w1_of(s, m), tile_t[:, b, :], start=True, stop=True).then_inc(sem["up_ps"], 1)
                    if not (final and u == tiles_turn - 1):
                        transpose_tile(g + 1, 1 - b)
                    pe.wait_ge(sem["act_ready"], g * KT + KT)
                    past(pe, sem["exp_out_ready"], g - 1)
                    for r in range(SUB):
                        for k in range(KT):
                            last = mm(down_banks[b][:, r * P:(r + 1) * P], act_h[:, b, k, r * P:(r + 1) * P], w2_of(s, k),
                                      start=(k == 0), stop=(k == KT - 1))
                    last.then_inc(sem["down_ps"], 1)

            turns(pe, E1 // 2, turn)

        def experts_act(act):
            def turn(pair, first, final):
                for u in range(tiles_turn):
                    g, b, s = pair * tiles_turn + u, u % 2, u // tiles_per
                    for m in range(KT):
                        act.wait_ge(sem["up_ps"], g * KT + m + 1)
                        if m == 0:
                            past(act, sem["down_ps"], g - 1)
                        nc.scalar.activation(act_h[:, b, m, :], up_banks[m][:, :], ACT.Gelu, bias=b1_of(s, m)).then_inc(sem["act_ready"], 1)

            act.wait_ge(w_loaded[0], 16)
            act.wait_ge(w_loaded[1], 16)
            turns(act, E1 // 2, turn)

        def experts_dve(dve):
            def take_tile(g, b):
                dve.wait_ge(sem["slot_t_ps"], g + 1)
                past(dve, sem["up_ps"], (g - 1) * KT)
                nc.vector.tensor_copy(tile_t[:, b, :], turn_banks[b][:, :]).then_inc(sem["slot_t_ready"], 1)

            take_tile(0, 0)

            def turn(pair, first, final):
                for u in range(tiles_turn):
                    g, b, s = pair * tiles_turn + u, u % 2, u // tiles_per
                    if not (final and u == tiles_turn - 1):
                        take_tile(g + 1, 1 - b)
                    dve.wait_ge(sem["down_ps"], g + 1)
                    past(dve, exp_stored[b], (g - b) * 8)
                    b2 = b2_of(s).unsqueeze(1).to_broadcast([P, SUB, P])
                    nc.vector.tensor_tensor(tile_out[:, b, :, :], down_banks[b][:, :].rearrange("p (r c) -> p r c", r=SUB), b2,
                                            ALU.add).then_inc(sem["exp_out_ready"], 1)

            turns(dve, E1 // 2, turn)

        def last_sp(sp):
            sp.wait_ge(sem["rows_stored"], 16 * B)

            def turn(pair, first, final):
                for s in range(2):
                    row = pair * 2 + s
                    past(sp, sem["y_out_ready"], row - 1)
                    sp.dma_start(y_rows[:, s, :, :], rows[row]).then_inc(rows_loaded[s], 16)
                    if not (first and s == 0):
                        store(row - 1, 1 - s)

            def store(row, s):
                sp.wait_ge(sem["y_out_ready"], row + 1)
                sp.dma_start(out[row].rearrange("(c p) n -> p c n", p=P), y_out[:, s, :, :]).then_inc(out_stored[s], 16)

            turns(sp, B // 2, turn)
            store(B - 1, 1)
            for s in range(2):
                sp.wait_ge(out_stored[s], 16 * (B // 2))

        def last_pool(pool):
            def gather(row, s):
                past(pool, sem["comb_ready"], row - 1)
                pool.wait_ge(sem["pick_ready"], row + 1)
                pool.sem_inc(sem["pool_passed"], 1)
                for n in range(2 * SUB):
                    nc.gpsimd.indirect_dma_start(
                        got[:, s, n, :], None, slots_out, bass.IndirectOffsetOnAxis(ap=pick[:, s, n:n + 1], axis=0),
                        bounds_check=SLOTS - 1, oob_is_err=False).then_inc(gathered[s], 16)

            for s in range(2):
                pool.wait_ge(exp_stored[s], 16 * (E1 * tiles_per // 2))
            gather(0, 0)
            gather(1, 1)

            def turn(pair, first, final):
                for s in range(2):
                    row = pair * 2 + s
                    pool.wait_ge(sem["last_var_ready"], row + 1)
                    nc.gpsimd.tensor_tensor(last_rstd[:, s, :], last_var[:, s, :], powers[:, 0, 0:SUB], ALU.pow).then_inc(sem["last_rstd_ready"], 1)
                    if not final:
                        gather(row + 2, s)

            turns(pool, B // 2, turn)

        def last_dve(dve):
            v = nc.vector

            def take_picks(row, s):
                if isinstance(row, int):
                    at = slice(row * SUB * 2, (row + 1) * SUB * 2)
                else:
                    at = bass.ds(row * (SUB * 2), SUB * 2)
                v.tensor_copy(pick_gate[:, s, :], gate_all[:, at])
                v.tensor_copy(pick[:, s, :], slot_all[:, at]).then_inc(sem["pick_ready"], 1)

            def combine(row, s, pair):
                dve.wait_ge(gathered[s], pair * 16 * 2 * SUB + 16 * 2 * SUB)
                dve.wait_ge(rows_loaded[s], pair * 16 + 16)
                dve.wait_ge(sem["pick_ready"], row + 1)
                for n in range(2):
                    for c in range(SUB):
                        ins = v.scalar_tensor_tensor(y_rows[:, s, c, :], got[:, s, 2 * c + n, :], pick_gate[:, s, 2 * c + n:2 * c + n + 1],
                                                     y_rows[:, s, c, :], ALU.mult, ALU.add)
                        if n == 0 and c == SUB - 1:
                            ins.then_inc(sem["comb_half"], 1)
                            dve.wait_ge(sem["comb_half"], row + 1)
                ins.then_inc(sem["comb_ready"], 1)
                dve.wait_ge(sem["comb_ready"], row + 1)
                for c in range(SUB):
                    ins = v.bn_stats(bn[:, c, :], y_rows[:, s, c, :])
                ins.then_inc(sem["bn_ready"], 1)
                dve.wait_ge(sem["bn_ready"], row + 1)
                dve.sem_inc(sem["dve_passed"], 1)
                for c in range(SUB):
                    ins = v.bn_aggr(mean_var[:, s, c, :], bn[:, c, :])
                ins.then_inc(sem["mean_ready"], 1)
                dve.wait_ge(sem["mean_ready"], row + 1)
                v.tensor_scalar(last_var[:, s, :], mean_var[:, s, :, 1], EPS, None, ALU.add).then_inc(sem["last_var_ready"], 1)

            def normalise(row, s, pair):
                dve.wait_ge(sem["last_rstd_ready"], row + 1)
                past(dve, out_stored[s], pair * 16)
                for c in range(SUB):
                    ins = v.tensor_scalar(y_out[:, s, c, :], y_rows[:, s, c, :], mean_var[:, s, c, 0:1], last_rstd[:, s, c:c + 1],
                                          ALU.subtract, ALU.mult)
                ins.then_inc(sem["y_out_ready"], 1)

            take_picks(0, 0)
            take_picks(1, 1)

            def turn(pair, first, final):
                for s in range(2):
                    row = pair * 2 + s
                    combine(row, s, pair)
                    if not final:
                        take_picks(row + 2, s)
                    if s == 1:
                        normalise(row - 1, 0, pair)
                    elif not first:
                        normalise(row - 1, 1, pair - 1)

            turns(dve, B // 2, turn, peeled=2)
            normalise(B - 1, 1, B // 2 - 1)

        block = ctx.enter_context(nc.Block())

        ROUTER_STEPS = 27
        ROUTE_STEPS = 30

        LIVE = [(0, (1, 0, 0, 0)), (1, (1, 1, 0, 0)), (2, (1, 1, 1, 0)), (3, (1, 1, 1, 1)), None,
                (B, (0, 1, 1, 1)), (B + 1, (0, 0, 1, 1)), (B + 2, (0, 0, 0, 1))]
        STEPS = 17
        OFFSET = (0, 0, 0, 0)
        ORDER = (0, 1, 2, 3)

        def pipeline(eng, stages):
            def turn(i, live):
                for step in range(STEPS):
                    for lag in ORDER:
                        if live[lag]:
                            stages[lag](step - OFFSET[lag], i - lag)

            for entry in LIVE:
                if entry is None:
                    with eng.Fori(4, B) as i:
                        turn(i, (1, 1, 1, 1))
                else:
                    turn(*entry)

        @block.sync
        def _(sp):
            sp.dma_start(par[:, :], params).then_inc(sem["params_in"], 16)
            sp.dma_start(mask[:, :, :], masks).then_inc(sem["masks_in"], 16)
            sp.wait_ge(sem["cleared"], 1)
            zero_src = zeros[:, :]
            zero_dst = slots_in.rearrange("(n p r) c -> n p (r c)", p=P, r=16)
            for n in range(SLOTS // (P * 16)):
                sp.dma_start(zero_dst[n], zero_src).then_inc(sem["zeroed_slots"], 16)

            def mix(step, j):
                if step == 0:
                    sp.wait_ge(sem["mixed_ready"], MIXES * j)
                    sp.dma_start(x_in[:, 1:T + 1], x_t[j]).then_inc(sem["x_in_loaded"], 16)

            def wkv(step, j):
                if step == 1:
                    sp.wait_ge(sem["o_ps"], j)
                    sp.dma_start(x_res[:, :], x_t[j]).then_inc(sem["x_res_loaded"], 16)

            def ffn(step, j):
                pass

            def gru(step, j):
                if step == 8:
                    sp.wait_ge(sem["rows_ready"], j + 1)
                    sp.dma_start(rows[j], x3_rows[:, :, :]).then_inc(sem["rows_stored"], 16)

            pipeline(sp, (mix, wkv, ffn, gru))
            experts_sp(sp)
            last_sp(sp)

        @block.tensor
        def _(pe):
            mm = pe.matmul

            def columns(ps, width, src, rhs):
                for c in range(SUB):
                    last = mm(ps[:, c * width:(c + 1) * width], src[:, c * P:(c + 1) * P], rhs, start=True, stop=True)
                return last

            def broadcast(ps, stat, width):
                w = P // width
                for c in range(SUB):
                    for h in range(width):
                        lhs = stat[:, c * width + h:c * width + h + 1].to_broadcast([P, w])
                        last = mm(ps[h * w:(h + 1) * w, c * P:(c + 1) * P], lhs, p("ident"), start=True, stop=True)
                return last

            pe.wait_ge(sem["params_in"], 16)
            mm(mix0[:, 0:P], p("wo"), p("centre"), start=True, stop=True)
            mm(mix0[:, P:2 * P], p("fv_raw"), p("centre"), start=True, stop=False)
            mm(mix0[:, P:2 * P], p("ident"), p("centre"), start=False, stop=True)
            for n in range(2):
                mm(mix0[:, (2 + n) * P:(3 + n) * P], p("f_w2", n * P, (n + 1) * P), p("centre"), start=True, stop=True)
            mm(mix1[0:E0, 0:P], p("f_b2"), p("centre"), start=True, stop=True)
            mm(mix1[:, P:P + 1], p("centre"), p("f_bv"), start=True, stop=True).then_inc(sem["setup_pe"], 1)

            def mix(step, j):
                if step == 2:
                    pe.wait_ge(sem["gate_ready"], j)
                    pe.wait_ge(sem["value_ready"], 3 * j)
                    pe.wait_ge(sem["x_mixed_ready"], j + 1)
                    mm(mix0[:, :], p("lora_a", 0, P), x_mixed[:, :], start=True, stop=True)
                    mm(mix1[0:RANK, :], p("lora_a", P), x_mixed[:, :], start=True, stop=True).then_inc(sem["lora_ps"], 1)
                if 3 <= step <= 7:
                    f = step - 3
                    ps = (mix0, mix1)[f % 2]
                    if f == 0:
                        pe.wait_ge(sem["lora_ready"], 2 * j + 2)
                    if f >= 2:
                        pe.wait_ge(sem["mixed_part"], MIXES * j + f - 1)
                    if f < 4:
                        lhs, rhs = p("lora_b")[f * RANK:(f + 1) * RANK], lora[f * RANK:(f + 1) * RANK, :]
                    else:
                        lhs, rhs = p("lora_b4", parts=RANK), lora4[:, :]
                    mm(ps[:, :], lhs, rhs, start=True, stop=True).then_inc(sem["miu_ps"], 1)
                if step == 8:
                    pe.wait_ge(sem["mixed_part"], MIXES * j + 5)
                    pe.wait_ge(sem["mixed_ready"], MIXES * j + 1)
                    mm(mix0[0:TD, :], p("td_a"), mixed[:, 0, :], start=True, stop=True).then_inc(sem["td_ps"], 1)
                if step == 9:
                    pe.wait_ge(sem["td_ready"], j + 1)
                    mm(mix0[:, :], p("td_b", parts=TD), td_hid[:, :], start=True, stop=True).then_inc(sem["w_ps"], 1)
                    pe.wait_ge(sem["mixed_ready"], MIXES * j + 2)
                    mm(mix1[:, :], p("wk"), mixed[:, 1, :], start=True, stop=True).then_inc(sem["k_ps"], 1)
                if step == 11:
                    pe.wait_ge(sem["exp_w_ready"], j + 1)
                    pe.wait_ge(sem["mixed_ready"], MIXES * j + 4)
                    mm(mix0[:, :], p("wr"), mixed[:, 3, :], start=True, stop=True).then_inc(sem["r_ps"], 1)
                if step == 13:
                    pe.wait_ge(sem["key_ready"], j + 1)
                    for c in range(SUB):
                        last = mm(mix1[:, c * P:(c + 1) * P], mixed[:, 2, c * P:(c + 1) * P], p("wv"), start=True, stop=True)
                    last.then_inc(sem["v_ps"], 1)
                if step == 14:
                    pe.wait_ge(sem["recep_ready"], 2 * j + 2)
                    pe.wait_ge(sem["mixed_ready"], MIXES * j + 5)
                    mm(mix0[:, :], p("wg"), mixed[:, 4, :], start=True, stop=True).then_inc(sem["g_ps"], 1)

            def wkv(step, j):
                if step <= LEVELS:
                    right = recep_u if step == 0 else recep
                    if step == 0:
                        pe.wait_ge(sem["key_ready"], j + 1)
                        pe.wait_ge(sem["recep_ready"], 2 * j + 2)
                        pe.wait_ge(sem["x1_ready"], j)
                    elif step == 1:
                        pe.wait_ge(sem["att_copied"], (LEVELS + 1) * j + 1)
                    else:
                        pe.wait_ge(sem["att_copied"], (LEVELS + 1) * j + step)
                        pe.wait_ge(sem["level_scaled"], (LEVELS + 1) * j + step - 1)
                    pe.sem_inc(sem["pe_passed"], 1)
                    for c in range(SUB):
                        for h in range(HEADS):
                            for q in range(2):
                                tok = slice(c * P + q * 64, c * P + q * 64 + 64)
                                last = mm(by_head[q * 64:q * 64 + 64, h, c, :], key[h * 64:h * 64 + 64, tok],
                                          right[h * 64:h * 64 + 64, tok], start=True, stop=True)
                    last.then_inc(sem["level_ps"], 1)
                if step == 7:
                    pe.wait_ge(sem["att_copied"], (LEVELS + 1) * (j + 1))
                    pe.wait_ge(sem["level_scaled"], (LEVELS + 1) * j + LEVELS)
                    pe.sem_inc(sem["pe_passed"], 1)
                    for c in range(SUB):
                        for h in range(HEADS):
                            last = mm(by_head[0:64, h, c, :], key[h * 64:h * 64 + 64, c * P:c * P + 64],
                                      recep[h * 64:h * 64 + 64, c * P + 64:c * P + P], start=True, stop=True)
                    last.then_inc(sem["off_ps"], 1)
                if step == 8:
                    pe.wait_ge(sem["off_ready"], j + 1)
                    pe.wait_ge(sem["level_scaled"], (LEVELS + 1) * (j + 1))
                    for c in range(SUB - 1):
                        last = pe.transpose(wkv0[:, c * P:(c + 1) * P], key[:, c * P:(c + 1) * P], p("ident"))
                    last.then_inc(sem["key_t_ps"], 1)
                    pe.wait_ge(sem["value_ready"], 3 * j + 3)
                    for c in range(SUB):
                        for h in range(HEADS):
                            lane = slice(h * 64, h * 64 + 64)
                            first, second = slice(c * P, c * P + 64), slice(c * P + 64, c * P + P)
                            mm(wkv1[lane, first], value_lo[:, c, lane], att[:, h, c, :], start=(c == 0), stop=False, skip_group_check=True)
                            mm(wkv1[lane, second], value_hi[:, c, lane], att[:, h, c, :], start=False, stop=False, skip_group_check=True)
                            last = mm(wkv1[lane, second], value_lo[:, c, lane], att_off[:, h, c, :], start=False, stop=(c == 0),
                                      skip_group_check=True)
                    last.then_inc(sem["intra_ps"], 1)
                if step == 9:
                    pe.wait_ge(sem["key_rows_ready"], j + 1)
                    for c in range(SUB - 1):
                        last = mm(wkv0[:, c * P:(c + 1) * P], key_rows[:, c, :], value[:, c, :], start=True, stop=True)
                    last.then_inc(sem["kv_ps"], 1)
                if step == 10:
                    pe.wait_ge(sem["state_ready"], j + 1)
                    for c in range(1, SUB):
                        last = mm(wkv1[:, c * P:(c + 1) * P], state[:, c - 1, :], recep[:, c * P:(c + 1) * P],
                                  start=False, stop=True, skip_group_check=True)
                    last.then_inc(sem["y_ps"], 1)
                if step == 11:
                    pe.wait_ge(sem["y_ready"], j + 1)
                    mm(wkv0[:, :], p("group_centre"), y_sb[:, :], start=True, stop=True).then_inc(sem["gn_cen_ps"], 1)
                if step == 12:
                    pe.wait_ge(sem["gn_sq_ready"], j + 1)
                    columns(wkv1, HEADS, wkv_sq, p("group_var")).then_inc(sem["gn_var_ps"], 1)
                if step == 13:
                    pe.wait_ge(sem["gn_cen_ready"], j + 1)
                    pe.wait_ge(sem["gn_rstd_ready"], j + 1)
                    broadcast(wkv0, gn_rstd, HEADS).then_inc(sem["gn_bc_ps"], 1)
                if step == 14:
                    pe.wait_ge(sem["x_res_loaded"], 16 * (j + 1))
                    pe.wait_ge(sem["gated_ready"], j + 1)
                    mm(wkv0[:, :], p("centre"), x_res[:, :], start=True, stop=False)
                    mm(wkv0[:, :], c_wo, gated[:, :], start=False, stop=True).then_inc(sem["o_ps"], 1)
                if step == 15:
                    pe.wait_ge(sem["ln1_sq_ready"], j + 1)
                    columns(wkv1, 1, wkv_sq, p("mean_col", 0, 1)).then_inc(sem["ln1_var_ps"], 1)
                if step == 16:
                    pe.wait_ge(sem["ln1_cen_ready"], j + 1)
                    pe.wait_ge(sem["ln1_rstd_ready"], j + 1)
                    broadcast(wkv0, ln1_rstd, 1).then_inc(sem["ln1_bc_ps"], 1)

            def ffn(step, j):
                if step == 0:
                    pe.wait_ge(sem["x2_ready"], j)
                    pe.wait_ge(sem["x1_ready"], j + 1)
                    mm(ffn0[:, :], p("fv"), x1[:, :], start=True, stop=True).then_inc(sem["val_ps"], 1)
                if step == 1:
                    pe.wait_ge(sem["val_ready"], j + 1)
                    w = E0 * (1 + PROTO)
                    columns(ffn1, w, val, p("f_router")).then_inc(sem["router_ps"], 1)
                if step in (3, 5):
                    n = (step - 3) // 2
                    if n == 1:
                        pe.wait_ge(sem["h_read"], 4 * j + 2)
                    mm(ffn0[:, :], p("f_w1", n * P, (n + 1) * P), val[:, :], start=True, stop=True).then_inc(sem["h_ps"], 1)
                if step == 8:
                    pe.wait_ge(sem["expert_w_ready"], j + 1)
                    for c in range(SUB):
                        last = pe.transpose(ffn1[0:E0, c * P:(c + 1) * P], expert_w[:, c, :], p("ident"))
                    last.then_inc(sem["wt_ps"], 1)
                if step == 9:
                    pe.wait_ge(sem["h_read"], 4 * j + 4)
                    pe.wait_ge(sem["wt_ready"], j + 1)
                    for n, ps in enumerate((ffn0, ffn1)):
                        mm(ps[:, :], p("spread", n * P, (n + 1) * P, parts=E0), expert_wt[:, :],
                           start=True, stop=True).then_inc(sem["spread_ps"], 1)
                if step == 11:
                    pe.wait_ge(sem["hid_ready"], 2 * j + 2)
                    mm(ffn0[:, :], c_fv, x1[:, :], start=True, stop=False)
                    mm(ffn0[:, :], c_b2[:, :], expert_wt[:, :], start=False, stop=False)
                    mm(ffn0[:, :], c_w2[0], hid[:, 0, :], start=False, stop=False)
                    mm(ffn0[:, :], c_w2[1], hid[:, 1, :], start=False, stop=True).then_inc(sem["delta_ps"], 1)
                if step == 12:
                    pe.wait_ge(sem["ln2_sq_ready"], j + 1)
                    columns(ffn1, 1, ffn_sq, p("mean_col", 0, 1)).then_inc(sem["ln2_var_ps"], 1)
                if step == 13:
                    pe.wait_ge(sem["ln2_cen_ready"], j + 1)
                    pe.wait_ge(sem["ln2_rstd_ready"], j + 1)
                    broadcast(ffn0, ln2_rstd, 1).then_inc(sem["ln2_bc_ps"], 1)

            def gru(step, j):
                if step == 0:
                    pe.wait_ge(sem["rows_ready"], j)
                    pe.wait_ge(sem["slots_ready"], j)
                    pe.wait_ge(sem["x2_ready"], j + 1)
                    mm(gru0[:, :], p("wz"), x2[:, :], start=True, stop=True).then_inc(sem["z_ps"], 1)
                    mm(gru1[:, :], p("wh"), x2[:, :], start=True, stop=True).then_inc(sem["t_ps"], 1)
                if step == 3:
                    pe.wait_ge(sem["z_read"], j + 1)
                    pe.wait_ge(sem["hidden_ready"], j + 1)
                    mm(gru0[:, :], p("centre"), x2[:, :], start=True, stop=False)
                    mm(gru0[:, :], c_quarter, hidden[:, :], start=False, stop=True).then_inc(sem["g_out_ps"], 1)
                if step == 4:
                    pe.wait_ge(sem["t_read"], 2 * j + 2)
                    pe.wait_ge(sem["ln3_sq_ready"], j + 1)
                    columns(gru1, 1, gru_sq, p("mean_col", 0, 1)).then_inc(sem["ln3_var_ps"], 1)
                if step == 5:
                    pe.wait_ge(sem["ln3_cen_ready"], j + 1)
                    pe.wait_ge(sem["ln3_rstd_ready"], j + 1)
                    broadcast(gru0, ln3_rstd, 1).then_inc(sem["ln3_bc_ps"], 1)
                if step == 6:
                    pe.wait_ge(sem["x3_ready"], j + 1)
                    columns(gru1, E1, x3, p("e_router")).then_inc(sem["logits_ps"], 1)
                    for c in range(SUB):
                        last = pe.transpose(gru0[:, c * P:(c + 1) * P], x3[:, c * P:(c + 1) * P], p("ident"))
                    last.then_inc(sem["rows_ps"], 1)
                if step == 12:
                    pe.wait_ge(sem["chosen_ready"], j + 1)
                    mm(gru1[:, 0:SUB * E1], p("upper"), chosen[:, :, :].rearrange("p c e -> p (c e)"), start=True, stop=False)
                    mm(gru1[:, 0:SUB * E1], p("ones"), seen[:, 0:SUB, :].rearrange("p c e -> p (c e)"),
                       start=False, stop=True).then_inc(sem["rank_ps"], 1)

            pipeline(pe, (mix, wkv, ffn, gru))
            experts_pe(pe)

        @block.scalar
        def _(act):
            def f(out, in_, func, **kw):
                return nc.scalar.activation(out, in_, func, **kw)

            act.wait_ge(sem["params_in"], 16)
            f(sig_alpha, p("alpha"), ACT.Tanh, scale=0.5).then_inc(sem["alpha_tanh"], 1)

            def mix(step, j):
                if step == 2:
                    act.wait_ge(sem["lora_ps"], j + 1)
                    f(lora[:, :], mix0[:, :], ACT.Tanh).then_inc(sem["lora_ready"], 1)
                    f(lora4[:, :], mix1[0:RANK, :], ACT.Tanh).then_inc(sem["lora_ready"], 1)
                if step == 8:
                    act.wait_ge(sem["td_ps"], j + 1)
                    f(td_hid[:, :], mix0[0:TD, :], ACT.Tanh).then_inc(sem["td_ready"], 1)
                if step == 10:
                    act.wait_ge(sem["w_ps"], j + 1)
                    f(exp_w[:, :], mix0[:, :], ACT.Exp, bias=p("td_miu")).then_inc(sem["exp_w_ready"], 1)
                    act.wait_ge(sem["exp_w_ready"], j + 1)
                    act.wait_ge(sem["level_scaled"], (LEVELS + 1) * j)
                    f(decay[:, :], exp_w[:, :], ACT.Exp, scale=-1.0).then_inc(sem["decay_ready"], 1)
                if step == 12:
                    act.wait_ge(sem["k_ps"], j + 1)
                    act.wait_ge(sem["y_ps"], j)
                    f(key[:, :], mix1[:, :], ACT.Copy).then_inc(sem["key_ready"], 1)
                    act.wait_ge(sem["r_ps"], j + 1)
                    f(recep[:, :], mix0[:, :], ACT.Copy).then_inc(sem["recep_ready"], 1)
                    f(recep_u[:, :], mix0[:, :], ACT.Identity, scale=p("bonus")).then_inc(sem["recep_ready"], 1)
                if step == 14:
                    act.wait_ge(sem["v_ps"], j + 1)
                    for dst, lane in ((value, slice(0, P)), (value_lo, slice(0, 64)), (value_hi, slice(64, P))):
                        f(dst[lane, :, :].rearrange("p c n -> p (c n)"), mix1[lane, :], ACT.Copy).then_inc(sem["value_ready"], 1)
                if step == 15:
                    act.wait_ge(sem["g_ps"], j + 1)
                    f(tanh_g[:, :], mix0[:, :], ACT.Tanh, scale=0.5).then_inc(sem["tanh_g_ready"], 1)

            def wkv(step, j):
                if step == 7:
                    act.wait_ge(sem["off_ps"], j + 1)
                    f(att_off[0:64, :, :, :], by_head[0:64], ACT.Copy).then_inc(sem["off_ready"], 1)
                if step == 8:
                    act.wait_ge(sem["key_t_ps"], j + 1)
                    f(key_rows[:, :, :].rearrange("p c n -> p (c n)"), wkv0[:, 0:(SUB - 1) * P], ACT.Copy).then_inc(sem["key_rows_ready"], 1)
                if step == 10:
                    act.wait_ge(sem["y_ps"], j + 1)
                    f(y_sb[:, :], wkv1[:, :], ACT.Copy).then_inc(sem["y_ready"], 1)
                if step == 11:
                    act.wait_ge(sem["gn_cen_ps"], j + 1)
                    f(wkv_sq[:, :], wkv0[:, :], ACT.Square).then_inc(sem["gn_sq_ready"], 1)
                    f(wkv_cen[:, :], wkv0[:, :], ACT.Copy).then_inc(sem["gn_cen_ready"], 1)
                if step == 14:
                    act.wait_ge(sem["o_ps"], j + 1)
                    f(wkv_sq[:, :], wkv0[:, :], ACT.Square).then_inc(sem["ln1_sq_ready"], 1)
                    f(wkv_cen[:, :], wkv0[:, :], ACT.Copy).then_inc(sem["ln1_cen_ready"], 1)

            def ffn(step, j):
                if step == 0:
                    act.wait_ge(sem["val_ps"], j + 1)
                    f(val[:, :], ffn0[:, :], ACT.Identity, bias=p("f_bv")).then_inc(sem["val_ready"], 1)
                if step == 1:
                    act.wait_ge(sem["router_step"], ROUTER_STEPS * j + 1)
                    routed = ffn1[:, 0:SUB * E0 * (1 + PROTO)].rearrange("p (c w) -> p c w", c=SUB)
                    f(proto_sq[:, :, :], routed[:, :, E0:], ACT.Square).then_inc(sem["proto_sq_ready"], 1)
                if step in (4, 6):
                    n = (step - 4) // 2
                    act.wait_ge(sem["h_ps"], 2 * j + n + 1)
                    f(tanh_h[:, n, :], ffn0[:, :], ACT.Tanh, scale=0.5, bias=half_b1[:, n:n + 1]).then_inc(sem["h_read"], 1)
                    f(half_h[:, n, :], ffn0[:, :], ACT.Identity, scale=0.5, bias=half_b1[:, n:n + 1]).then_inc(sem["h_read"], 1)
                if step == 7:
                    act.wait_ge(sem["ffn_gap_ready"], j + 1)
                    f(ffn_top.ratio[:, :], ffn_top.gap[:, :], ACT.Exp).then_inc(sem["ffn_ratio_ready"], 1)
                if step == 8:
                    act.wait_ge(sem["wt_ps"], j + 1)
                    f(expert_wt[:, :], ffn1[0:E0, :], ACT.Copy).then_inc(sem["wt_ready"], 1)
                if step == 11:
                    act.wait_ge(sem["delta_ps"], j + 1)
                    f(ffn_sq[:, :], ffn0[:, :], ACT.Square, bias=c_bv).then_inc(sem["ln2_sq_ready"], 1)
                    f(ffn_cen[:, :], ffn0[:, :], ACT.Identity, bias=c_bv).then_inc(sem["ln2_cen_ready"], 1)

            def gru(step, j):
                if step == 0:
                    act.wait_ge(sem["z_ps"], j + 1)
                    f(tanh_z[:, :], gru0[:, :], ACT.Tanh, scale=0.5, bias=half_bz).then_inc(sem["z_read"], 1)
                    act.wait_ge(sem["t_ps"], j + 1)
                    f(tanh_t[:, :], gru1[:, :], ACT.Tanh, scale=0.5, bias=half_bh).then_inc(sem["t_read"], 1)
                    f(lin_t[:, :], gru1[:, :], ACT.Identity, scale=2.0, bias=double_bh).then_inc(sem["t_read"], 1)
                if step == 3:
                    act.wait_ge(sem["g_out_ps"], j + 1)
                    f(gru_sq[:, :], gru0[:, :], ACT.Square).then_inc(sem["ln3_sq_ready"], 1)
                    f(gru_cen[:, :], gru0[:, :], ACT.Copy).then_inc(sem["ln3_cen_ready"], 1)
                if step == 6:
                    act.wait_ge(sem["rows_ps"], j + 1)
                    act.wait_ge(sem["scattered"], 16 * 2 * SUB * j)
                    act.wait_ge(sem["rows_stored"], 16 * j)
                    f(x3_rows[:, :, :].rearrange("p c n -> p (c n)"), gru0[:, :], ACT.Copy).then_inc(sem["rows_ready"], 1)
                if step == 11:
                    act.wait_ge(sem["gru_gap_ready"], j + 1)
                    f(gru_top.ratio[:, :], gru_top.gap[:, :], ACT.Exp).then_inc(sem["gru_ratio_ready"], 1)

            act.wait_ge(sem["setup_done"], 1)
            pipeline(act, (mix, wkv, ffn, gru))
            experts_act(act)

        def top2_pick(link, s, top):
            desc = p("descend").rearrange("p (c e) -> p c e", c=SUB)
            for n, src in ((0, s), (1, top.rest[:, :, :])):
                link(nc.vector.tensor_reduce(top.best[:, n, :], src, AX_X, ALU.max))
                link(nc.vector.tensor_tensor(top.equal[:, :, :], src, top.best[:, n, :].unsqueeze(2).to_broadcast([P, SUB, E0]), ALU.is_equal))
                link(nc.vector.tensor_tensor(top.equal[:, :, :], top.equal[:, :, :], desc, ALU.mult))
                link(nc.vector.tensor_reduce(top.rank[:, :], top.equal[:, :, :], AX_X, ALU.max))
                link(nc.vector.tensor_tensor(top.hot[:, n, :, :], desc, top.rank[:, :].unsqueeze(2).to_broadcast([P, SUB, E0]), ALU.is_equal))
                if n == 0:
                    link(nc.vector.scalar_tensor_tensor(top.rest[:, :, :], top.hot[:, 0, :, :], -BIG, s, ALU.mult, ALU.add))

        @block.vector
        def _(dve):
            v = nc.vector
            tt, ts, stt = v.tensor_tensor, v.tensor_scalar, v.scalar_tensor_tensor

            def linker(signal, base):
                count = [0]

                def link(ins):
                    count[0] += 1
                    ins.then_inc(signal, 1)
                    dve.wait_ge(signal, base + count[0])
                return link, count

            setup, _ = linker(sem["setup_dve"], 0)
            v.memset(zeros[:, :], 0.0).then_inc(sem["cleared"], 1)
            setup(v.memset(x_in[:, 0:1], 0.0))
            setup(v.memset(att[:, :, :, :], 0.0))
            setup(v.memset(att_off[:, :, :, :], 0.0))
            setup(v.memset(value_lo[:, :, :], 0.0))
            setup(v.memset(value_hi[:, :, :], 0.0))
            setup(v.memset(state[:, :, :], 0.0))
            setup(v.memset(seen[:, :, :], 0.0))
            setup(v.memset(powers[:, 0, :], -0.5))
            setup(v.memset(powers[:, 1, :], 0.5))
            dve.wait_ge(sem["params_in"], 16)
            setup(ts(half_beta, p("gn_beta"), 0.5, None, ALU.mult))
            setup(ts(half_b1, p("f_b1"), 0.5, None, ALU.mult))
            setup(ts(half_bz, p("b_z"), 0.5, None, ALU.mult))
            setup(ts(half_bh, p("b_h"), 0.5, None, ALU.mult))
            setup(ts(double_bh, p("b_h"), 2.0, None, ALU.mult))
            setup(ts(c_quarter, p("centre"), 0.25, None, ALU.mult))
            dve.wait_ge(sem["alpha_tanh"], 1)
            setup(ts(small[:, 8:9], sig_alpha, 0.5, 0.5, ALU.mult, ALU.add))
            setup(ts(router_scale[:, 0, :], p("f_gr"), float(E0) ** 0.5, None, ALU.mult))
            setup(ts(router_scale[:, 1, :], p("f_gc"), small[:, 8:9], float(E0) ** 0.5, ALU.mult, ALU.mult))
            setup(stt(router_shift[:, :], p("f_bc"), small[:, 8:9], p("f_br"), ALU.mult, ALU.add))
            dve.wait_ge(sem["setup_pe"], 1)
            setup(v.tensor_copy(folded[:, 0:4 * P], mix0[:, :]))
            setup(v.tensor_copy(c_b2[:, :], mix1[0:E0, 0:P]))
            setup(v.tensor_copy(c_bv, mix1[:, P:P + 1]))
            dve.wait_ge(sem["masks_in"], 16)
            v.memset(small[:, 9:10], 0.0).then_inc(sem["setup_done"], 1)

            def mix(step, j):
                if step == 0:
                    dve.wait_ge(sem["x_in_loaded"], 16 * (j + 1))
                    tt(dx[:, :], x_in[:, 0:T], x_in[:, 1:T + 1], ALU.subtract).then_inc(sem["dx_ready"], 1)
                if step == 1:
                    dve.wait_ge(sem["dx_ready"], j + 1)
                    stt(x_mixed[:, :], dx[:, :], p("miu_x"), x_in[:, 1:T + 1], ALU.mult, ALU.add).then_inc(sem["x_mixed_ready"], 1)
                if 3 <= step <= 7:
                    f = step - 3
                    dve.wait_ge(sem["miu_ps"], MIXES * j + f + 1)
                    if f == 0:
                        dve.wait_ge(sem["g_ps"], j)
                    stt(mixed[:, f, :], (mix0, mix1)[f % 2][:, :], p("lam", f, f + 1), dx[:, :], ALU.add, ALU.mult).then_inc(sem["mixed_part"], 1)
                if step == 15:
                    dve.wait_ge(sem["tanh_g_ready"], j + 1)
                    dve.wait_ge(sem["gated_ready"], j)
                    stt(gate[:, :], tanh_g[:, :], 1.0, mix0[:, :], ALU.add, ALU.mult).then_inc(sem["gate_ready"], 1)

            def scale_level(j, level):
                b = 1 << level
                n = T // b
                off = 0 if level <= 1 else T - (T >> (level - 1))
                tot = decay[:, :] if level == 0 else total[:, off:off + n]
                nxt_off = 0 if level == 0 else T - (T >> level)
                halves = tot.rearrange("p (n two) -> p n two", two=2)
                left = halves[:, :, 0:1].to_broadcast([P, n // 2, b]) if b > 1 else halves[:, :, 0:1]
                right = halves[:, :, 1:2].to_broadcast([P, n // 2, b]) if b > 1 else halves[:, :, 1:2]
                r = recep[:, :].rearrange("p (n two b) -> p n two b", two=2, b=b)[:, :, 1, :]
                k = key[:, :].rearrange("p (n two b) -> p n two b", two=2, b=b)[:, :, 0, :]
                if level == 0:
                    dve.wait_ge(sem["decay_ready"], j + 1)
                    dve.wait_ge(sem["level_ps"], (LEVELS + 1) * j + 2)
                elif level < LEVELS:
                    dve.wait_ge(sem["level_ps"], (LEVELS + 1) * j + level + 2)
                    dve.wait_ge(sem["level_scaled"], (LEVELS + 1) * j + level)
                else:
                    dve.wait_ge(sem["off_ps"], j + 1)
                    dve.wait_ge(sem["level_scaled"], (LEVELS + 1) * j + level)
                tt(total[:, nxt_off:nxt_off + n // 2], halves[:, :, 0], halves[:, :, 1], ALU.mult)
                tt(r, r, left, ALU.mult)
                tt(k, k, right, ALU.mult).then_inc(sem["level_scaled"], 1)

            def wkv(step, j):
                if step <= LEVELS:
                    dve.wait_ge(sem["level_ps"], (LEVELS + 1) * j + step + 1)
                    if step == 0:
                        dve.wait_ge(sem["intra_ps"], j)
                    else:
                        dve.wait_ge(sem["att_copied"], (LEVELS + 1) * j + step)
                    dve.sem_inc(sem["dve_passed"], 1)
                    v.copy_predicated(att[:, :, :, :], mask[:, step, :].unsqueeze(1).unsqueeze(1).to_broadcast([P, HEADS, SUB, 64]),
                                      by_head).then_inc(sem["att_copied"], 1)
                    if step >= 1:
                        scale_level(j, step - 1)
                if step == 7:
                    scale_level(j, LEVELS)
                if step == 9:
                    dve.wait_ge(sem["kv_ps"], j + 1)
                    tot_off = T - (T >> LEVELS)
                    for c in range(SUB - 1):
                        if c:
                            dve.wait_ge(sem["state_step"], 2 * (SUB - 2) * j + 2 * c)
                        for h in range(HEADS):
                            lane = slice(h * 64, h * 64 + 64)
                            kv = wkv0[lane, c * P + h * 64:c * P + h * 64 + 64]
                            if c == 0:
                                ins = v.tensor_copy(state[lane, 0, lane], kv)
                            else:
                                ins = stt(state[lane, c, lane], state[lane, c - 1, lane], total[lane, tot_off + c:tot_off + c + 1],
                                          kv, ALU.mult, ALU.add)
                            if c < SUB - 2:
                                ins.then_inc(sem["state_step"], 1)
                            elif h == HEADS - 1:
                                ins.then_inc(sem["state_ready"], 1)
                if step == 12:
                    dve.wait_ge(sem["gn_var_ps"], j + 1)
                    ts(gn_var[:, :], wkv1[:, 0:SUB * HEADS], 4 * EPS * HEADS, None, ALU.add).then_inc(sem["gn_var_ready"], 1)
                if step == 13:
                    dve.wait_ge(sem["gn_bc_ps"], j + 1)
                    tt(gated[:, :], wkv_cen[:, :], wkv0[:, :], ALU.mult).then_inc(sem["gated_step"], 1)
                    dve.wait_ge(sem["gated_step"], 2 * j + 1)
                    dve.wait_ge(sem["gate_ready"], j + 1)
                    ts(gated[:, :], gated[:, :], p("gn_gamma"), half_beta, ALU.mult, ALU.add).then_inc(sem["gated_step"], 1)
                    dve.wait_ge(sem["gated_step"], 2 * j + 2)
                    tt(gated[:, :], gated[:, :], gate[:, :], ALU.mult).then_inc(sem["gated_ready"], 1)
                if step == 15:
                    dve.wait_ge(sem["ln1_var_ps"], j + 1)
                    ts(ln1_var[:, :], wkv1[:, 0:SUB], EPS, None, ALU.add).then_inc(sem["ln1_var_ready"], 1)
                if step == 16:
                    dve.wait_ge(sem["ln1_bc_ps"], j + 1)
                    dve.wait_ge(sem["delta_ps"], j)
                    tt(x1[:, :], wkv_cen[:, :], wkv0[:, :], ALU.mult).then_inc(sem["x1_ready"], 1)

            def ffn(step, j):
                if step == 1:
                    dve.wait_ge(sem["router_ps"], j + 1)
                    routed = ffn1[:, 0:SUB * E0 * (1 + PROTO)].rearrange("p (c w) -> p c w", c=SUB)
                    bg = p("f_bg").unsqueeze(1).to_broadcast([P, SUB, E0])
                    tt(rc[:, 0, :, :], routed[:, :, 0:E0], bg, ALU.add).then_inc(sem["router_step"], 1)
                if step == 2:
                    link, _ = linker(sem["router_step"], j * ROUTER_STEPS + 1)
                    dve.wait_ge(sem["proto_sq_ready"], j + 1)
                    link(v.tensor_reduce(norm_sq[:, :, :], proto_sq[:, :, :].rearrange("p c (e q) -> p c e q", q=PROTO), AX_X, ALU.add))
                    ts(rc_sq[:, 1, :, :], norm_sq[:, :, :], 1.0 / PROTO, None, ALU.mult).then_inc(sem["norm_sq_ready"], 1)
                if step == 3:
                    link, _ = linker(sem["router_step"], j * ROUTER_STEPS + 2)
                    dve.wait_ge(sem["norm_ready"], j + 1)
                    link(v.tensor_reduce(rc_sum[:, :], rc[:, :, :, :].rearrange("p k c e -> p (k c) e"), AX_X, ALU.add))
                    mean = rc_sum[:, :].unsqueeze(2).to_broadcast([P, 2 * SUB, E0])
                    flat = rc[:, :, :, :].rearrange("p k c e -> p (k c) e")
                    link(stt(rc_cen[:, :, :, :].rearrange("p k c e -> p (k c) e"), mean, -1.0 / E0, flat, ALU.mult, ALU.add))
                    link(tt(rc_sq[:, :, :, :], rc_cen[:, :, :, :], rc_cen[:, :, :, :], ALU.mult))
                    link(v.tensor_reduce(rc_sum[:, :], rc_sq[:, :, :, :].rearrange("p k c e -> p (k c) e"), AX_X, ALU.add))
                    ts(rc_sum[:, :], rc_sum[:, :], E0 * EPS, None, ALU.add).then_inc(sem["rc_sq_ready"], 1)
                if step == 5:
                    link, _ = linker(sem["router_step"], j * ROUTER_STEPS + 6)
                    dve.wait_ge(sem["rc_rstd_ready"], j + 1)
                    rstd = rc_rstd[:, :].unsqueeze(2).to_broadcast([P, 2 * SUB, E0])
                    link(tt(rc_norm[:, :, :, :].rearrange("p k c e -> p (k c) e"), rc_cen[:, :, :, :].rearrange("p k c e -> p (k c) e"), rstd, ALU.mult))
                    for k in range(2):
                        g = router_scale[:, k:k + 1, :].to_broadcast([P, SUB, E0])
                        link(tt(rc_norm[:, k, :, :], rc_norm[:, k, :, :], g, ALU.mult))
                    link(tt(rc_norm[:, 0, :, :], rc_norm[:, 0, :, :], rc_norm[:, 1, :, :], ALU.add))
                    link(tt(rc_norm[:, 0, :, :], rc_norm[:, 0, :, :], router_shift[:, :].unsqueeze(1).to_broadcast([P, SUB, E0]), ALU.add))
                    top2_pick(link, rc_norm[:, 0, :, :], ffn_top)
                    tt(ffn_top.gap[:, :], ffn_top.best[:, 1, :], ffn_top.best[:, 0, :], ALU.subtract).then_inc(sem["ffn_gap_ready"], 1)
                if step == 7:
                    link, _ = linker(sem["router_step"], j * ROUTER_STEPS + 22)
                    dve.wait_ge(sem["ffn_ratio_ready"], j + 1)
                    shares(link, ffn_top)
                    for n in range(2):
                        w = ffn_top.share[:, :, n:n + 1].to_broadcast([P, SUB, E0])
                        link(tt(ffn_top.hot[:, n, :, :], ffn_top.hot[:, n, :, :], w, ALU.mult))
                    tt(expert_w[:, :, :], ffn_top.hot[:, 0, :, :], ffn_top.hot[:, 1, :, :], ALU.add).then_inc(sem["expert_w_ready"], 1)
                if step in (4, 6):
                    n = (step - 4) // 2
                    dve.wait_ge(sem["h_read"], 4 * j + 2 * n + 2)
                    stt(tanh_h[:, n, :], tanh_h[:, n, :], 1.0, half_h[:, n, :], ALU.add, ALU.mult).then_inc(sem["silu_ready"], 1)
                if step == 10:
                    dve.wait_ge(sem["silu_ready"], 2 * j + 2)
                    for n, ps in enumerate((ffn0, ffn1)):
                        dve.wait_ge(sem["spread_ps"], 2 * j + n + 1)
                        tt(hid[:, n, :], tanh_h[:, n, :], ps[:, :], ALU.mult).then_inc(sem["hid_ready"], 1)
                if step == 12:
                    dve.wait_ge(sem["ln2_var_ps"], j + 1)
                    ts(ln2_var[:, :], ffn1[:, 0:SUB], EPS, None, ALU.add).then_inc(sem["ln2_var_ready"], 1)
                if step == 13:
                    dve.wait_ge(sem["ln2_bc_ps"], j + 1)
                    dve.wait_ge(sem["g_out_ps"], j)
                    tt(x2[:, :], ffn_cen[:, :], ffn0[:, :], ALU.mult).then_inc(sem["x2_ready"], 1)

            def shares(link, top):
                link(ts(top.den[:, :], top.ratio[:, :], 1.0, None, ALU.add))
                link(v.reciprocal(top.share[:, :, 0], top.den[:, :]))
                link(tt(top.share[:, :, 1], top.ratio[:, :], top.share[:, :, 0], ALU.mult))

            def gru(step, j):
                if step == 1:
                    link, _ = linker(sem["gru_step"], 4 * j)
                    dve.wait_ge(sem["t_read"], 2 * j + 2)
                    dve.wait_ge(sem["z_read"], j + 1)
                    link(tt(lin_t[:, :], lin_t[:, :], tanh_t[:, :], ALU.max))
                    link(ts(keep_z[:, :], tanh_z[:, :], -0.5, 0.5, ALU.mult, ALU.add))
                    link(ts(take_z[:, :], tanh_z[:, :], 1.0, None, ALU.add))
                    link(stt(take_z[:, :], lin_t[:, :], 1.0, take_z[:, :], ALU.add, ALU.mult))
                if step == 2:
                    dve.wait_ge(sem["gru_step"], 4 * j + 4)
                    v.tensor_tensor_scan(hidden[:, :], keep_z[:, :], take_z[:, :], 0.0, ALU.mult, ALU.add).then_inc(sem["hidden_ready"], 1)
                if step == 4:
                    dve.wait_ge(sem["ln3_var_ps"], j + 1)
                    ts(ln3_var[:, :], gru1[:, 0:SUB], EPS, None, ALU.add).then_inc(sem["ln3_var_ready"], 1)
                if step == 5:
                    dve.wait_ge(sem["ln3_bc_ps"], j + 1)
                    tt(x3[:, :], gru_cen[:, :], gru0[:, :], ALU.mult).then_inc(sem["x3_ready"], 1)
                if step == 7:
                    link, _ = linker(sem["route_step"], j * ROUTE_STEPS)
                    dve.wait_ge(sem["logits_ps"], j + 1)
                    br = p("e_br").unsqueeze(1).to_broadcast([P, SUB, E1])
                    link(tt(logits[:, :, :], gru1[:, 0:SUB * E1].rearrange("p (c e) -> p c e", c=SUB), br, ALU.add))
                    top2_pick(link, logits[:, :, :], gru_top)
                    tt(gru_top.gap[:, :], gru_top.best[:, 1, :], gru_top.best[:, 0, :], ALU.subtract).then_inc(sem["gru_gap_ready"], 1)
                    link(tt(chosen[:, :, :], gru_top.hot[:, 0, :, :], gru_top.hot[:, 1, :, :], ALU.add))
                    link(v.tensor_copy(seen[:, 0, :], seen[:, SUB, :]))
                    for c in range(SUB):
                        ins = tt(seen[:, c + 1, :], seen[:, c, :], chosen[:, c, :], ALU.add)
                        if c < SUB - 1:
                            link(ins)
                    ins.then_inc(sem["chosen_ready"], 1)
                if step == 13:
                    link, _ = linker(sem["route_step"], j * ROUTE_STEPS + 17)
                    dve.wait_ge(sem["gru_ratio_ready"], j + 1)
                    shares(link, gru_top)
                    dve.wait_ge(sem["rank_ps"], j + 1)
                    rank = gru1[:, 0:SUB * E1].rearrange("p (c e) -> p c e", c=SUB)
                    link(ts(over[:, :, :], rank, float(CAP), float(SLOTS), ALU.is_ge, ALU.mult))
                    link(tt(slot_of[:, :, :], rank, p("slot_base").rearrange("p (c e) -> p c e", c=SUB), ALU.add))
                    link(tt(slot_of[:, :, :], slot_of[:, :, :], over[:, :, :], ALU.max))
                    for n in range(2):
                        link(tt(pick_tmp[:, :, n, :], slot_of[:, :, :], gru_top.hot[:, n, :, :], ALU.mult))
                    link(v.tensor_reduce(slot_f[:, :, :], pick_tmp[:, :, :, :], AX_X, ALU.add))
                    dve.wait_ge(sem["scattered"], 16 * 2 * SUB * j)
                    link(v.tensor_copy(slot_scatter[:, :], slot_f[:, :, :].rearrange("p c n -> p (c n)")))
                    link(ts(kept[:, :, :], slot_f[:, :, :], float(SLOTS), None, ALU.is_lt))
                    link(tt(slot_f[:, :, :], slot_f[:, :, :], kept[:, :, :], ALU.mult))
                    row = slice(j * SUB * 2, j * SUB * 2 + SUB * 2) if isinstance(j, int) else bass.ds(j * (SUB * 2), SUB * 2)
                    link(v.tensor_copy(slot_all[:, row], slot_f[:, :, :].rearrange("p c n -> p (c n)")))
                    tt(gate_all[:, row], gru_top.share[:, :, :].rearrange("p c n -> p (c n)"),
                       kept[:, :, :].rearrange("p c n -> p (c n)"), ALU.mult).then_inc(sem["slots_ready"], 1)

            pipeline(dve, (mix, wkv, ffn, gru))
            experts_dve(dve)
            last_dve(dve)

        @block.gpsimd
        def _(pool):
            g = nc.gpsimd
            pool.wait_ge(sem["setup_done"], 1)
            pool.wait_ge(sem["zeroed_slots"], 16 * (SLOTS // (P * 16)))

            def power(out, in_, which, n):
                return g.tensor_tensor(out, in_, powers[:, which, 0:n], ALU.pow)

            def mix(step, j):
                if 4 <= step <= 8:
                    f = step - 4
                    pool.wait_ge(sem["mixed_part"], MIXES * j + f + 1)
                    g.tensor_tensor(mixed[:, f, :], mixed[:, f, :], x_in[:, 1:T + 1], ALU.add).then_inc(sem["mixed_ready"], 1)

            def wkv(step, j):
                if step == 12:
                    pool.wait_ge(sem["gn_var_ready"], j + 1)
                    power(gn_rstd[:, :], gn_var[:, :], 0, SUB * HEADS).then_inc(sem["gn_rstd_ready"], 1)
                if step == 15:
                    pool.wait_ge(sem["ln1_var_ready"], j + 1)
                    power(ln1_rstd[:, :], ln1_var[:, :], 0, SUB).then_inc(sem["ln1_rstd_ready"], 1)

            def ffn(step, j):
                if step == 2:
                    pool.wait_ge(sem["norm_sq_ready"], j + 1)
                    power(rc[:, 1, :, :].rearrange("p c e -> p (c e)"), rc_sq[:, 1, :, :].rearrange("p c e -> p (c e)"), 1,
                          SUB * E0).then_inc(sem["norm_ready"], 1)
                if step == 4:
                    pool.wait_ge(sem["rc_sq_ready"], j + 1)
                    power(rc_rstd[:, :], rc_sum[:, :], 0, 2 * SUB).then_inc(sem["rc_rstd_ready"], 1)
                if step == 12:
                    pool.wait_ge(sem["ln2_var_ready"], j + 1)
                    power(ln2_rstd[:, :], ln2_var[:, :], 0, SUB).then_inc(sem["ln2_rstd_ready"], 1)

            def gru(step, j):
                if step == 4:
                    pool.wait_ge(sem["ln3_var_ready"], j + 1)
                    power(ln3_rstd[:, :], ln3_var[:, :], 0, SUB).then_inc(sem["ln3_rstd_ready"], 1)
                if step == 16:
                    pool.wait_ge(sem["slots_ready"], j + 1)
                    pool.wait_ge(sem["rows_ready"], j + 1)
                    pool.sem_inc(sem["pool_passed"], 1)
                    for c in range(SUB):
                        for n in range(2):
                            g.indirect_dma_start(
                                slots_in, bass.IndirectOffsetOnAxis(ap=slot_scatter[:, 2 * c + n:2 * c + n + 1], axis=0),
                                x3_rows[:, c, :], None, bounds_check=SLOTS - 1, oob_is_err=False).then_inc(sem["scattered"], 16)

            pipeline(pool, (mix, wkv, ffn, gru))
            last_pool(pool)


def pack_params(a):
    import numpy as np

    def put(rows, width):
        full = np.zeros((P, width), np.float32)
        full[:rows.shape[0]] = rows
        return full

    def column(x):
        return np.asarray(x).reshape(-1, P).T

    def row(x):
        return np.broadcast_to(np.asarray(x).reshape(1, -1), (P, np.asarray(x).size))

    eye = np.eye(P, dtype=np.float32)
    head = np.arange(P) // HS
    same = (head[:, None] == head[None, :]).astype(np.float32)
    before = (np.arange(P)[:, None] < np.arange(P)[None, :]).astype(np.float32)
    group_var = (head[:, None] == np.arange(HEADS)[None, :]).astype(np.float32) * (4.0 / HS)
    spread = (np.arange(E0)[:, None] == (np.arange(2 * P) // INNER)[None, :]).astype(np.float32)
    lora_b = np.asarray(a["L0_attn_B_lora"])
    fields = {
        "ident": eye, "centre": (eye - 1.0 / P).astype(np.float32), "group_centre": (eye - same / HS).astype(np.float32),
        "upper": before, "ones": np.ones((P, P), np.float32), "mean_col": np.full((P, 2), 1.0 / P, np.float32),
        "group_var": group_var, "spread": put(spread, 2 * P),
        "descend": row(np.tile(np.arange(E0, 0, -1), SUB).astype(np.float32)),
        "slot_base": row(np.tile(np.arange(E1) * CAP, SUB).astype(np.float32)),
        "lora_a": a["L0_attn_A_lora"], "lora_b": lora_b[0:4].reshape(P, P), "lora_b4": put(lora_b[4], P),
        "td_a": a["L0_attn_td_A"], "td_b": put(np.asarray(a["L0_attn_td_B"]), P),
        "wk": np.asarray(a["L0_attn_Wk"]).T, "wv": np.asarray(a["L0_attn_Wv"]).T, "wr": np.asarray(a["L0_attn_Wr"]).T,
        "wg": np.asarray(a["L0_attn_Wg"]).T, "wo": a["L0_attn_Wo"],
        "fv": np.asarray(a["L0_ffn_Wv"]).T, "fv_raw": a["L0_ffn_Wv"],
        "f_router": np.concatenate([np.asarray(a["L0_ffn_Wg"]), np.asarray(a["L0_ffn_Wp"]).reshape(E0 * PROTO, P)]).T,
        "f_w1": np.asarray(a["L0_ffn_W1"]).reshape(2 * P, P).T,
        "f_w2": np.asarray(a["L0_ffn_W2"]).transpose(1, 0, 2).reshape(P, 2 * P), "f_b2": np.asarray(a["L0_ffn_b2"]).T,
        "wz": np.asarray(a["L1_attn_W_z"]).T, "wh": np.asarray(a["L1_attn_W_h"]).T, "e_router": a["L1_ffn_Wr"],
        "miu_x": column(a["L0_attn_miu_x"]), "lam": column(a["L0_attn_lambda_"]), "td_miu": column(a["L0_attn_td_miu"]),
        "bonus": column(a["L0_attn_u"]), "gn_gamma": column(a["L0_attn_gn_gamma"]), "gn_beta": column(a["L0_attn_gn_beta"]),
        "f_bv": column(a["L0_ffn_bv"]), "f_b1": column(a["L0_ffn_b1"]), "b_z": column(a["L1_attn_b_z"]), "b_h": column(a["L1_attn_b_h"]),
        "f_bg": row(a["L0_ffn_bg"]), "f_gr": row(a["L0_ffn_g_r"]), "f_br": row(a["L0_ffn_b_r"]), "f_gc": row(a["L0_ffn_g_c"]),
        "f_bc": row(a["L0_ffn_b_c"]), "alpha": row(a["L0_ffn_alpha"]), "e_br": row(a["L1_ffn_br"]),
    }
    for name, width in FIELDS:
        assert np.asarray(fields[name]).shape == (P, width), name
    return np.ascontiguousarray(np.concatenate([np.asarray(fields[name]) for name, _ in FIELDS], axis=1))


def pack_experts(a):
    import numpy as np

    w1 = np.asarray(a["L1_ffn_W1"])
    w2 = np.asarray(a["L1_ffn_W2"]).reshape(E1, KT, P, P).transpose(0, 2, 1, 3).reshape(E1, P, HID)
    b1 = np.asarray(a["L1_ffn_b1"]).reshape(E1, KT, P).transpose(0, 2, 1)
    b2 = np.broadcast_to(np.asarray(a["L1_ffn_b2"])[:, None, :], (E1, P, P))
    return np.ascontiguousarray(np.concatenate([w1, w2, b1, b2], axis=2))


def level_masks():
    import numpy as np

    src = (np.arange(P) % 64)[:, None]
    dst = np.arange(64)[None, :]
    found = [src == dst]
    for level in range(LEVELS):
        b = 1 << level
        found.append((src // (2 * b) == dst // (2 * b)) & (src % (2 * b) < b) & (dst % (2 * b) >= b))
    return np.ascontiguousarray(np.stack(found, axis=1).astype(np.uint32))


def kernel(**inputs):
    import numpy as np
    import concourse.bacc as bacc
    from concourse.bass_utils import run_bass_kernel_spmd as run

    nc = bacc.Bacc("TRN2", target_bir_lowering=False, num_devices=1)
    arrays = {
        "x_t": np.ascontiguousarray(np.asarray(inputs["L0_attn_x"]).transpose(0, 2, 1)),
        "params": pack_params(inputs),
        "masks": level_masks(),
        "experts": pack_experts(inputs),
    }
    args = [nc.dram_tensor(n, a.shape, mybir.dt.from_np(a.dtype), kind="ExternalInput").ap() for n, a in arrays.items()]
    args.append(nc.dram_tensor("out_0_dram", (B, T, P), F32, kind="ExternalOutput").ap())
    build_network(nc, *args)
    r = run(nc, [arrays], core_ids=[0])
    return r.results[0]["out_0_dram"]
```

```python
from contextlib import ExitStack

import concourse.bass as bass
from concourse import mybir

ALU = mybir.AluOpType
ACT = mybir.ActivationFunctionType
F32 = mybir.dt.float32
F32R = mybir.dt.float32r
U32 = mybir.dt.uint32
AX_X = mybir.AxisListType.X

P = 128
T = 512
B = 16
SUB = T // P
HEADS, HS = 2, 64
RANK = 32
MIXES = 5
TD = 64
E0, INNER, PROTO = 8, 32, 8
E1, HID = 8, 512
CAP = B * T * 2 // E1
SLOTS = E1 * CAP
LEVELS = 6
TILE = 512
DEEP = 4
EPS = 1e-5
BIG = 1.0e30

FIELDS = [
    ("centre", P), ("spread", 2 * P), ("ident", P), ("group_centre", P), ("upper", P), ("ones", P), ("mean_col", 2),
    ("group_var", HEADS), ("descend", SUB * E0), ("slot_base", SUB * E1), ("dest_base", 2 * SUB),
    ("lora_a", RANK * MIXES), ("lora_b", P), ("lora_b4", P), ("td_a", TD), ("td_b", P),
    ("wk", P), ("wv", P), ("wr", P), ("wg", P), ("wo", P),
    ("fv", P), ("fv_raw", P), ("f_router", E0 * (1 + PROTO)), ("f_w1", 2 * P), ("f_w2", 2 * P), ("f_b2", 3 * E0),
    ("wz", P), ("wh", P), ("e_router", E1), ("low_rows", 1),
    ("miu_x", 1), ("lam", MIXES), ("td_miu", 1), ("bonus", 1), ("gn_gamma", 1), ("gn_beta", 1),
    ("f_bv", 1), ("f_b1", 2), ("b_z", 1), ("b_h", 1),
    ("f_bg", E0), ("f_gr", E0), ("f_br", E0), ("f_gc", E0), ("f_bc", E0), ("alpha", 1), ("e_br", E1),
]
WIDTH = sum(w for _, w in FIELDS)
ROW = P + 2
KT = HID // P
EXPERT_WIDTH = 2 * HID + KT + 1


def build_network(nc, x_t, params, masks, experts, out):
    with ExitStack() as ctx:
        buffers = [ctx]

        def sb(name, shape, dt=F32):
            return buffers[-1].enter_context(nc.sbuf_tensor(name, shape, dt))

        def sems(text):
            return {n: ctx.enter_context(nc.semaphore(n)) for n in text.split()}

        slots_in = nc.dram_tensor("slots_in", [SLOTS, ROW], F32, kind="Internal").ap()
        parts = nc.dram_tensor("parts", [B * P * 2 * SUB, P], F32, kind="Internal").ap()

        par = sb("par", [P, WIDTH])
        col, at = {}, 0
        for name, w in FIELDS:
            col[name] = (at, w)
            at += w

        def p(name, lo=0, hi=None, parts=P):
            start, w = col[name]
            return par[0:parts, start + lo:start + (w if hi is None else hi)]

        mask = sb("mask", [P, LEVELS + 1, 64], U32)
        folded = sb("folded", [P, 5 * P])
        c_wo, c_fv = folded[:, 0:P], folded[:, P:2 * P]
        c_w2 = [folded[:, (2 + n) * P:(3 + n) * P] for n in range(2)]
        c_quarter = folded[:, 4 * P:5 * P]
        exact = sb("exact", [P, 3 * P], F32R)
        centre_exact, spread_exact = exact[:, 0:P], [exact[0:3 * E0, (1 + n) * P:(2 + n) * P] for n in range(2)]
        c_b2 = sb("c_b2", [3 * E0, P], F32R)
        c_b2_high = sb("c_b2_high", [3 * E0, P], F32R)
        small = sb("small", [P, 64])
        half_beta, c_bv = small[:, 0:1], small[:, 1:2]
        half_b1, half_bz, half_bh, double_bh = small[:, 2:4], small[:, 4:5], small[:, 5:6], small[:, 6:7]
        sig_alpha = small[:, 7:8]
        router_scale = sb("router_scale", [P, 2, E0])
        router_shift = sb("router_shift", [P, E0])
        powers = sb("powers", [P, 2, 64])
        empty_slot = sb("empty_slot", [P, ROW])

        no_output = sb("no_output", [P, 2 * SUB * P])

        x3_kept = sb("x3_kept", [P, B, SUB, P])
        expert_par = sb("expert_par", [P, 2, EXPERT_WIDTH])
        tiles_per = CAP // TILE
        tiles_turn = 2 * tiles_per
        w_high, w_low = sb("w_high", [P, 2, 2 * HID], F32R), sb("w_low", [P, 2, 2 * HID], F32R)
        tile_in = sb("tile_in", [P, 2, SUB, ROW])

        buffers.append(ctx.enter_context(ExitStack()))

        x_in = sb("x_in", [P, T + 1])
        dx = sb("dx", [P, T])
        x_mixed = sb("x_mixed", [P, T])
        lora = sb("lora", [P, T])
        lora4 = sb("lora4", [RANK, T])
        mixed = sb("mixed", [P, MIXES, T])
        td_hid = sb("td_hid", [TD, T])
        exp_w = sb("exp_w", [P, T])
        tanh_g = sb("tanh_g", [P, T])
        key = sb("key", [P, T])
        recep = sb("recep", [P, T])
        recep_u = sb("recep_u", [P, T])
        decay = sb("decay", [P, T])
        value = sb("value", [P, SUB, P])
        value_lo = sb("value_lo", [P, SUB, P])
        value_hi = sb("value_hi", [P, SUB, P])
        gate = sb("gate", [P, T])
        total = sb("total", [P, T])
        att = sb("att", [P, HEADS, SUB, 64])
        att_off = sb("att_off", [P, HEADS, SUB, 64])
        key_rows = sb("key_rows", [P, SUB - 1, P])
        state = sb("state", [P, SUB - 1, P])
        y_sb = sb("y_sb", [P, T])
        wkv_sq = sb("wkv_sq", [P, T])
        wkv_cen = sb("wkv_cen", [P, T])
        gated = sb("gated", [P, T])
        gn_var, gn_rstd = sb("gn_var", [P, SUB * HEADS]), sb("gn_rstd", [P, SUB * HEADS])
        ln1_var, ln1_rstd = sb("ln1_var", [P, SUB]), sb("ln1_rstd", [P, SUB])
        x_res = sb("x_res", [P, T])
        x_res_high, x_res_low = sb("x_res_high", [P, T], F32R), sb("x_res_low", [P, T], F32R)
        x1 = sb("x1", [P, T])
        val = sb("val", [P, T])
        proto_sq = sb("proto_sq", [P, SUB, E0 * PROTO])
        rc = sb("rc", [P, 2, SUB, E0])
        rc_sum = sb("rc_sum", [P, 2 * SUB])
        rc_cen = sb("rc_cen", [P, 2, SUB, E0])
        rc_sq = sb("rc_sq", [P, 2, SUB, E0])
        rc_rstd = sb("rc_rstd", [P, 2 * SUB])
        rc_norm = sb("rc_norm", [P, 2, SUB, E0])
        norm_sq = sb("norm_sq", [P, SUB, E0])
        expert_w = sb("expert_w", [P, SUB, E0])
        expert_w_high = sb("expert_w_high", [P, SUB, E0], F32R)
        expert_w3 = sb("expert_w3", [P, SUB, 3 * E0])
        expert_wt = sb("expert_wt", [3 * E0, T], F32R)
        tanh_h = sb("tanh_h", [P, 2, T])
        half_h = sb("half_h", [P, 2, T])
        hid = sb("hid", [P, 2, T])
        ffn_sq = sb("ffn_sq", [P, T])
        ffn_cen = sb("ffn_cen", [P, T])
        ln2_var, ln2_rstd = sb("ln2_var", [P, SUB]), sb("ln2_rstd", [P, SUB])
        x2 = sb("x2", [P, T])
        tanh_z = sb("tanh_z", [P, T])
        tanh_t = sb("tanh_t", [P, T])
        lin_t = sb("lin_t", [P, T])
        keep_z = sb("keep_z", [P, T])
        take_z = sb("take_z", [P, T])
        hidden = sb("hidden", [P, T])
        gru_sq = sb("gru_sq", [P, T])
        gru_cen = sb("gru_cen", [P, T])
        ln3_var, ln3_rstd = sb("ln3_var", [P, SUB]), sb("ln3_rstd", [P, SUB])
        x3 = sb("x3", [P, T])
        x3_rows = sb("x3_rows", [P, 2, SUB, ROW])
        dest = sb("dest", [P, 2, SUB])
        logits = sb("logits", [P, SUB, E1])
        chosen = sb("chosen", [P, SUB, E1])
        seen = sb("seen", [P, SUB + 1, E1])
        over = sb("over", [P, SUB, E1])
        slot_of = sb("slot_of", [P, SUB, E1])
        pick_tmp = sb("pick_tmp", [P, SUB, 2, E1])
        slot_f = sb("slot_f", [P, SUB, 2])
        slot_scatter = sb("slot_scatter", [P, SUB * 2], U32)

        class Top2:

            def __init__(self, tag):
                self.best = sb(tag + "best", [P, 2, SUB])
                self.equal = sb(tag + "equal", [P, SUB, E0])
                self.rank = sb(tag + "rank", [P, SUB])
                self.hot = sb(tag + "hot", [P, 2, SUB, E0])
                self.rest = sb(tag + "rest", [P, SUB, E0])
                self.gap = sb(tag + "gap", [P, SUB])
                self.ratio = sb(tag + "ratio", [P, SUB])
                self.den = sb(tag + "den", [P, SUB])
                self.share = sb(tag + "share", [P, SUB, 2])

        ffn_top, gru_top = Top2("ffn_"), Top2("gru_")

        bank = {n: ctx.enter_context(nc.psum_tensor(n, [P, T], F32))
                for n in ("mix0", "mix1", "ffn0", "ffn1", "gru0", "gru1")}
        wkv_banks = ctx.enter_context(nc.psum_tensor("wkv_banks", [P, 2 * T], F32))
        wkv0, wkv1 = wkv_banks[:, 0:T], wkv_banks[:, T:2 * T]
        by_head = wkv_banks[:, :].rearrange("p (h n t) -> p h n t", h=HEADS, t=64)[:, :, 0:SUB, :]
        mix0, mix1 = bank["mix0"], bank["mix1"]
        ffn0, ffn1, gru0, gru1 = bank["ffn0"], bank["ffn1"], bank["gru0"], bank["gru1"]

        sem = sems(
            "passed params_in masks_in zeroed_slots zeroed_parts cleared alpha_tanh setup_dve setup_pe setup_done"
            " x_in_loaded dx_ready x_mixed_ready lora_ps lora_ready miu_ps mixed_part mixed_ready"
            " td_ps td_ready w_ps exp_w_ready decay_ready k_ps key_ready r_ps recep_ready v_ps value_ready g_ps tanh_g_ready gate_ready"
            " x_res_split x_res_loaded level_ps att_copied level_scaled off_ps off_ready key_t_ps key_rows_ready intra_ps"
            " kv_ps state_step state_ready y_ps y_ready gn_cen_ps gn_sq_ready gn_cen_ready gn_var_ps gn_var_ready gn_rstd_ready gn_bc_ps"
            " gated_step gated_ready o_ps ln1_sq_ready ln1_cen_ready ln1_var_ps ln1_var_ready ln1_rstd_ready ln1_bc_ps x1_ready"
            " val_ps val_ready router_ps proto_sq_ready router_step norm_sq_ready norm_ready rc_sq_ready rc_rstd_ready ffn_gap_ready ffn_ratio_ready"
            " expert_w_ready wt_ps wt_ready h_ps h_read silu_ready spread_ps hid_ready delta_ps ln2_sq_ready ln2_cen_ready"
            " ln2_var_ps ln2_var_ready ln2_rstd_ready ln2_bc_ps x2_ready"
            " z_ps t_ps z_read t_read gru_step hidden_ready g_out_ps ln3_sq_ready ln3_cen_ready ln3_var_ps ln3_var_ready ln3_rstd_ready"
            " ln3_bc_ps x3_ready logits_ps rows_ps rows_ready route_step gru_gap_ready gru_ratio_ready chosen_ready rank_ps"
            " slots_ready scattered"
            " w_loaded0 w_loaded1 w_high_ready w_split_ready act_high_ready tile_high_ready slots_loaded0 slots_loaded1 slot_t_ps slot_t_ready up_ps act_ready act_split_ready down_ps down_t_ready out_rows_ps exp_out_ready exp_stored0 exp_stored1"
            " parts_loaded0 parts_loaded1 parts_loaded2 parts_loaded3 pair_sum_ready comb_ready bn_ready mean_ready last_var_ready"
            " last_rstd_ready shift_ready y_out_ready out_stored0 out_stored1")

        buffers.pop().close()

        tile_high, tile_low = sb("tile_high", [P, 2, TILE], F32R), sb("tile_low", [P, 2, TILE], F32R)
        act_high, act_low = sb("act_high", [P, 2, KT, TILE], F32R), sb("act_low", [P, 2, KT, TILE], F32R)

        def w1_of(half, s, m):
            return half[:, s, m * P:(m + 1) * P]

        def w2_of(half, s, k):
            return half[:, s, HID + k * P:HID + (k + 1) * P]

        def b1_of(s, m):
            return expert_par[:, s, 2 * HID + m:2 * HID + m + 1]

        def b2_of(s):
            return expert_par[:, s, 2 * HID + KT:2 * HID + KT + 1]

        tile_dest = sb("tile_dest", [P, tiles_turn, SUB], U32)
        tile_gate = sb("tile_gate", [P, tiles_turn, SUB])
        down_t = sb("down_t", [P, 2, TILE])
        act_h = sb("act_h", [P, 2, KT, TILE])
        tile_out = sb("tile_out", [P, 2, SUB, P])
        part_in = sb("part_in", [P, DEEP, 2, SUB * P])
        pair_sum = sb("pair_sum", [P, 2, SUB * P])
        shift = sb("shift", [P, DEEP, SUB])
        y_rows = sb("y_rows", [P, DEEP, SUB, P])
        y_out = sb("y_out", [P, 2, SUB, P])
        bn = sb("bn", [P, SUB, 6])
        mean_var = sb("mean_var", [P, DEEP, SUB, 2])
        last_var, last_rstd = sb("last_var", [P, DEEP, SUB]), sb("last_rstd", [P, DEEP, SUB])

        parts_rows = parts.rearrange("(b p n) c -> b p (n c)", b=B, p=P)
        slot_tiles_in = slots_in.rearrange("(g p r) c -> g p r c", p=P, r=SUB)
        up_banks, down_bank, turn_banks = (wkv0, wkv1, ffn0, ffn1), gru0, (mix0, mix1)
        w_loaded, slots_loaded, exp_stored = (sem["w_loaded0"], sem["w_loaded1"]), (sem["slots_loaded0"], sem["slots_loaded1"]), (sem["exp_stored0"], sem["exp_stored1"])
        parts_loaded = [sem["parts_loaded%d" % n] for n in range(DEEP)]
        out_stored = (sem["out_stored0"], sem["out_stored1"])

        def past(eng, signal, value):
            if not (isinstance(value, int) and value <= 0):
                eng.wait_ge(signal, value)

        def turns(eng, count, turn, peeled=1):
            for n in range(peeled):
                turn(n, n == 0, False)
            with eng.Fori(peeled, count - 1) as n:
                turn(n, False, False)
            turn(count - 1, False, True)

        def experts_sp(sp):
            def weights(e, s):
                sp.dma_start(expert_par[:, s, :], experts[e]).then_inc(w_loaded[s], 16)

            def load(g, b):
                sp.dma_start(tile_in[:, b, :, :], slot_tiles_in[g]).then_inc(slots_loaded[b], 16)

            weights(0, 0)
            weights(1, 1)
            sp.wait_ge(sem["scattered"], 16 * 2 * SUB * B)
            load(0, 0)
            load(1, 1)

            def turn(pair, first, final):
                for u in range(tiles_turn):
                    g = pair * tiles_turn + u
                    if not (final and u >= tiles_turn - 2):
                        sp.wait_ge(sem["slot_t_ready"], g + 1)
                        load(g + 2, u % 2)
                    if u == 1 and not first:
                        sp.wait_ge(sem["down_t_ready"], g - 1)
                        weights(pair * 2 + 1, 1)
                    if u == tiles_per + 1 and not final:
                        sp.wait_ge(sem["down_t_ready"], g - 1)
                        weights(pair * 2 + 2, 0)

            turns(sp, E1 // 2, turn)

        def experts_pe(pe):
            mm = pe.matmul

            def transpose_tile(g, b):
                past(pe, sem["slot_t_ready"], g - 1)
                pe.wait_ge(slots_loaded[b], (g - b) * 8 + 16)
                for r in range(SUB):
                    last = pe.transpose(turn_banks[b][:, r * P:(r + 1) * P], tile_in[:, b, r, 0:P], p("ident"))
                last.then_inc(sem["slot_t_ps"], 1)

            def down(g, b, s):
                pe.wait_ge(sem["act_split_ready"], g * KT + KT)
                past(pe, sem["down_t_ready"], g)
                for k in range(KT):
                    mm(down_bank[:, :], w2_of(w_high, s, k), act_high[:, b, k, :], start=(k == 0), stop=False)
                    mm(down_bank[:, :], w2_of(w_high, s, k), act_low[:, b, k, :], start=False, stop=False)
                    last = mm(down_bank[:, :], w2_of(w_low, s, k), act_high[:, b, k, :], start=False, stop=(k == KT - 1))
                last.then_inc(sem["down_ps"], 1)

            def turn_back(g, b):
                pe.wait_ge(sem["down_t_ready"], g + 1)
                past(pe, sem["exp_out_ready"], g)
                for r in range(SUB):
                    last = pe.transpose(gru1[:, r * P:(r + 1) * P], down_t[:, b, r * P:(r + 1) * P], p("ident"))
                last.then_inc(sem["out_rows_ps"], 1)

            pe.wait_ge(sem["gate_ready"], B)
            pe.wait_ge(sem["x1_ready"], B)
            pe.wait_ge(sem["x2_ready"], B)
            pe.wait_ge(sem["rows_ready"], 3 * B)
            pe.wait_ge(sem["slots_ready"], B)
            transpose_tile(0, 0)

            def turn(pair, first, final):
                for u in range(tiles_turn):
                    g, b, s = pair * tiles_turn + u, u % 2, u // tiles_per
                    if u % tiles_per == 0:
                        pe.wait_ge(sem["w_split_ready"], pair * 2 + s + 1)
                    pe.wait_ge(sem["slot_t_ready"], g + 1)
                    for m in range(KT):
                        past(pe, sem["act_ready"], (g - 1) * KT + m + 1)
                        mm(up_banks[m][:, :], w1_of(w_high, s, m), tile_high[:, b, :], start=True, stop=False)
                        mm(up_banks[m][:, :], w1_of(w_high, s, m), tile_low[:, b, :], start=False, stop=False)
                        mm(up_banks[m][:, :], w1_of(w_low, s, m), tile_high[:, b, :], start=False, stop=True).then_inc(sem["up_ps"], 1)
                    if not (final and u == tiles_turn - 1):
                        transpose_tile(g + 1, 1 - b)
                    if not (first and u <= 1):
                        turn_back(g - 2, b)
                    if not (first and u == 0):
                        down(g - 1, 1 - b, (u - 1) // tiles_per % 2)

            turns(pe, E1 // 2, turn)
            final_tile = E1 * tiles_per - 1
            turn_back(final_tile - 1, 0)
            down(final_tile, 1, 1)
            turn_back(final_tile, 1)

        def experts_act(act):
            def high(g, b, m):
                act.wait_ge(sem["act_ready"], g * KT + m + 1)
                nc.scalar.copy(act_high[:, b, m, :], act_h[:, b, m, :]).then_inc(sem["act_high_ready"], 1)

            def add_bias(g, b, s):
                act.wait_ge(sem["down_ps"], g + 1)
                past(act, sem["out_rows_ps"], g - 1)
                nc.scalar.activation(down_t[:, b, :], down_bank[:, :], ACT.Identity, bias=b2_of(s)).then_inc(sem["down_t_ready"], 1)

            def weights_high(expert, s, loads):
                act.wait_ge(w_loaded[s], 16 * loads)
                past(act, sem["down_ps"], (expert - 1) * tiles_per)
                nc.scalar.copy(w_high[:, s, :], expert_par[:, s, 0:2 * HID]).then_inc(sem["w_high_ready"], 1)

            def turn(pair, first, final):
                for u in range(tiles_turn):
                    g, b, s = pair * tiles_turn + u, u % 2, u // tiles_per
                    for m in range(KT):
                        act.wait_ge(sem["up_ps"], g * KT + m + 1)
                        if m == 0:
                            past(act, sem["down_ps"], g - 1)
                        nc.scalar.activation(act_h[:, b, m, :], up_banks[m][:, :], ACT.Gelu, bias=b1_of(s, m)).then_inc(sem["act_ready"], 1)
                        if m >= 1:
                            high(g, b, m - 1)
                    high(g, b, KT - 1)
                    if not (first and u == 0):
                        add_bias(g - 1, 1 - b, (u - 1) // tiles_per % 2)
                    if u == 2:
                        weights_high(pair * 2 + 1, 1, pair + 1)
                    if u == tiles_per + 2 and not final:
                        weights_high(pair * 2 + 2, 0, pair + 2)

            weights_high(0, 0, 1)
            turns(act, E1 // 2, turn)
            add_bias(E1 * tiles_per - 1, 1, 1)

        def experts_dve(dve):
            v = nc.vector

            def take_tile(g, b, place):
                dve.wait_ge(sem["slot_t_ps"], g + 1)
                past(dve, sem["up_ps"], (g - 1) * KT)
                v.tensor_copy(tile_high[:, b, :], turn_banks[b][:, :]).then_inc(sem["tile_high_ready"], 1)
                past(dve, exp_stored[b], (g - b) * 32 - 192)
                v.tensor_copy(tile_dest[:, place, :], tile_in[:, b, :, P])
                v.tensor_copy(tile_gate[:, place, :], tile_in[:, b, :, P + 1])
                dve.wait_ge(sem["tile_high_ready"], g + 1)
                v.tensor_tensor(tile_low[:, b, :], turn_banks[b][:, :], tile_high[:, b, :], ALU.subtract).then_inc(sem["slot_t_ready"], 1)

            def low(g, b, m):
                dve.wait_ge(sem["act_high_ready"], g * KT + m + 1)
                v.tensor_tensor(act_low[:, b, m, :], act_h[:, b, m, :], act_high[:, b, m, :], ALU.subtract).then_inc(sem["act_split_ready"], 1)

            def weights_low(expert, s):
                dve.wait_ge(sem["w_high_ready"], expert + 1)
                v.tensor_tensor(w_low[:, s, :], expert_par[:, s, 0:2 * HID], w_high[:, s, :], ALU.subtract).then_inc(sem["w_split_ready"], 1)

            def gated_rows(g, b, place):
                dve.wait_ge(sem["out_rows_ps"], g + 1)
                past(dve, exp_stored[b], (g - b) * 32)
                gates = tile_gate[:, place, :].unsqueeze(2).to_broadcast([P, SUB, P])
                v.tensor_tensor(tile_out[:, b, :, :], gru1[:, :].rearrange("p (r c) -> p r c", r=SUB), gates,
                                ALU.mult).then_inc(sem["exp_out_ready"], 1)

            def turn(pair, first, final):
                for u in range(tiles_turn):
                    g, b = pair * tiles_turn + u, u % 2
                    low(g, b, 0)
                    low(g, b, 1)
                    if not (final and u == tiles_turn - 1):
                        take_tile(g + 1, 1 - b, (u + 1) % tiles_turn)
                    if not (first and u <= 1):
                        gated_rows(g - 2, b, (u - 2) % tiles_turn)
                    low(g, b, 2)
                    low(g, b, 3)
                    if u == 2:
                        weights_low(pair * 2 + 1, 1)
                    if u == tiles_per + 2 and not final:
                        weights_low(pair * 2 + 2, 0)

            weights_low(0, 0)
            take_tile(0, 0, 0)
            turns(dve, E1 // 2, turn)
            final_tile = E1 * tiles_per - 1
            gated_rows(final_tile - 1, 0, tiles_turn - 2)
            gated_rows(final_tile, 1, tiles_turn - 1)

        def experts_pool(pool):
            pool.wait_ge(sem["zeroed_parts"], 16 * B)

            def turn(pair, first, final):
                for u in range(tiles_turn):
                    g, b = pair * tiles_turn + u, u % 2
                    pool.wait_ge(sem["exp_out_ready"], g + 1)
                    pool.sem_inc(sem["passed"], 1)
                    for r in range(SUB):
                        nc.gpsimd.indirect_dma_start(
                            parts, bass.IndirectOffsetOnAxis(ap=tile_dest[:, u, r:r + 1], axis=0), tile_out[:, b, r, :], None,
                            bounds_check=B * P * 2 * SUB - 1, oob_is_err=False).then_inc(exp_stored[b], 16)

            turns(pool, E1 // 2, turn)

        def last_sp(sp):
            for s in range(2):
                sp.wait_ge(exp_stored[s], 64 * (E1 * tiles_per // 2))

            def turn(quad, first, final):
                for n in range(DEEP):
                    row = quad * DEEP + n
                    past(sp, sem["pair_sum_ready"], row - DEEP + 1)
                    sp.dma_start(part_in[:, n, :, :].rearrange("p k n -> p (k n)"), parts_rows[row]).then_inc(parts_loaded[n], 16)

            turns(sp, B // DEEP, turn)

        def last_pool(pool):
            def sum_pair(row, n):
                s = n % 2
                pool.wait_ge(parts_loaded[n], (row - n) * (16 // DEEP) + 16)
                past(pool, sem["comb_ready"], row - 1)
                nc.gpsimd.tensor_tensor(pair_sum[:, s, :], part_in[:, n, 0, :], part_in[:, n, 1, :], ALU.add).then_inc(sem["pair_sum_ready"], 1)

            sum_pair(0, 0)

            def turn(quad, first, final):
                for n in range(DEEP):
                    row = quad * DEEP + n
                    if not (final and n == DEEP - 1):
                        sum_pair(row + 1, (n + 1) % DEEP)
                    pool.wait_ge(sem["last_var_ready"], row + 1)
                    nc.gpsimd.tensor_tensor(last_rstd[:, n, :], last_var[:, n, :], powers[:, 0, 0:SUB], ALU.pow).then_inc(sem["last_rstd_ready"], 1)

            turns(pool, B // DEEP, turn)

        def last_dve(dve):
            v = nc.vector

            def statistics(row, n):
                dve.wait_ge(sem["pair_sum_ready"], row + 1)
                past(dve, sem["y_out_ready"], row - DEEP + 1)
                kept = x3_kept[:, row, :, :] if isinstance(row, int) else x3_kept[:, bass.ds(row, 1), :, :]
                kept = kept.rearrange("p c n -> p (c n)") if isinstance(row, int) else kept.rearrange("p o c n -> p (o c n)")
                v.tensor_tensor(y_rows[:, n, :, :].rearrange("p c n -> p (c n)"), pair_sum[:, n % 2, :], kept, ALU.add).then_inc(sem["comb_ready"], 1)
                dve.wait_ge(sem["comb_ready"], row + 1)
                for c in range(SUB):
                    ins = v.bn_stats(bn[:, c, :], y_rows[:, n, c, :])
                ins.then_inc(sem["bn_ready"], 1)
                dve.wait_ge(sem["bn_ready"], row + 1)
                dve.sem_inc(sem["passed"], 1)
                for c in range(SUB):
                    ins = v.bn_aggr(mean_var[:, n, c, :], bn[:, c, :])
                ins.then_inc(sem["mean_ready"], 1)
                dve.wait_ge(sem["mean_ready"], row + 1)
                v.tensor_scalar(last_var[:, n, :], mean_var[:, n, :, 1], EPS, None, ALU.add).then_inc(sem["last_var_ready"], 1)

            def shifts(row, n):
                dve.wait_ge(sem["last_rstd_ready"], row + 1)
                v.scalar_tensor_tensor(shift[:, n, :], mean_var[:, n, :, 0], -1.0, last_rstd[:, n, :], ALU.mult, ALU.mult).then_inc(sem["shift_ready"], 1)

            def turn(quad, first, final):
                for n in range(DEEP):
                    row = quad * DEEP + n
                    statistics(row, n)
                    if not (first and n == 0):
                        shifts(row - 1, (n - 1) % DEEP)

            turns(dve, B // DEEP, turn)
            shifts(B - 1, DEEP - 1)

        def last_act(act):
            def turn(quad, first, final):
                for n in range(DEEP):
                    row, s = quad * DEEP + n, n % 2
                    act.wait_ge(sem["shift_ready"], row + 1)
                    past(act, out_stored[s], (quad * 2 + n // 2) * 16)
                    for c in range(SUB):
                        ins = nc.scalar.activation(y_out[:, s, c, :], y_rows[:, n, c, :], ACT.Identity,
                                                   scale=last_rstd[:, n, c:c + 1], bias=shift[:, n, c:c + 1])
                    ins.then_inc(sem["y_out_ready"], 1)
                    act.wait_ge(sem["y_out_ready"], row + 1)
                    act.dma_start(out[row].rearrange("(c p) n -> p c n", p=P), y_out[:, s, :, :]).then_inc(out_stored[s], 16)

            turns(act, B // DEEP, turn)
            for s in range(2):
                act.wait_ge(out_stored[s], 16 * (B // 2))

        block = ctx.enter_context(nc.Block())

        ROUTER_STEPS = 27
        ROUTE_STEPS = 29

        LIVE = [(0, (1, 0, 0, 0)), (1, (1, 1, 0, 0)), (2, (1, 1, 1, 0)), (3, (1, 1, 1, 1)), None,
                (B, (0, 1, 1, 1)), (B + 1, (0, 0, 1, 1)), (B + 2, (0, 0, 0, 1))]
        STEPS = 17
        OFFSET = (0, 0, 0, 0)
        ORDER = (0, 1, 2, 3)
        PE_ORDER = ((3, 0, 2, 1), ORDER)

        def pipeline(eng, stages, order=(ORDER, ORDER)):
            def turn(i, live):
                for step in range(STEPS):
                    for lag in order[step > LEVELS]:
                        if live[lag]:
                            stages[lag](step - OFFSET[lag], i - lag)

            for entry in LIVE:
                if entry is None:
                    with eng.Fori(4, B) as i:
                        turn(i, (1, 1, 1, 1))
                else:
                    turn(*entry)

        @block.sync
        def _(sp):
            sp.dma_start(par[:, :], params).then_inc(sem["params_in"], 16)
            sp.dma_start(mask[:, :, :], masks).then_inc(sem["masks_in"], 16)
            empty_slots = slots_in.rearrange("(n p r) c -> n p r c", p=P, r=16)

            def mix(step, j):
                if step == 0:
                    sp.wait_ge(sem["mixed_ready"], MIXES * j)
                    sp.dma_start(x_in[:, 1:T + 1], x_t[j]).then_inc(sem["x_in_loaded"], 16)
                if step == 2:
                    sp.wait_ge(sem["cleared"], 2)
                    sp.dma_start(parts_rows[j], no_output[:, :]).then_inc(sem["zeroed_parts"], 16)
                    if isinstance(j, int) and j < 2:
                        half = SLOTS // (P * 16) // 2
                        for n in range(j * half, (j + 1) * half):
                            sp.dma_start(empty_slots[n], empty_slot[:, :].unsqueeze(1).to_broadcast([P, 16, ROW])).then_inc(sem["zeroed_slots"], 16)

            def wkv(step, j):
                if step == 1:
                    sp.wait_ge(sem["o_ps"], j)
                    sp.dma_start(x_res[:, :], x_t[j]).then_inc(sem["x_res_loaded"], 16)

            def ffn(step, j):
                pass

            def gru(step, j):
                pass

            pipeline(sp, (mix, wkv, ffn, gru))
            experts_sp(sp)
            last_sp(sp)

        @block.tensor
        def _(pe):
            mm = pe.matmul

            def columns(ps, width, src, rhs):
                for c in range(SUB):
                    last = mm(ps[:, c * width:(c + 1) * width], src[:, c * P:(c + 1) * P], rhs, start=True, stop=True)
                return last

            def broadcast(ps, stat, width):
                w = P // width
                for c in range(SUB):
                    for h in range(width):
                        lhs = stat[:, c * width + h:c * width + h + 1].to_broadcast([P, w])
                        last = mm(ps[h * w:(h + 1) * w, c * P:(c + 1) * P], lhs, p("ident"), start=True, stop=True)
                return last

            pe.wait_ge(sem["params_in"], 16)
            mm(mix0[:, 0:P], p("wo"), p("centre"), start=True, stop=True)
            mm(mix0[:, P:2 * P], p("fv_raw"), p("centre"), start=True, stop=False)
            mm(mix0[:, P:2 * P], p("ident"), p("centre"), start=False, stop=True)
            for n in range(2):
                mm(mix0[:, (2 + n) * P:(3 + n) * P], p("f_w2", n * P, (n + 1) * P), p("centre"), start=True, stop=True)
            mm(mix1[0:3 * E0, 0:P], p("f_b2"), p("centre"), start=True, stop=True)
            mm(mix1[:, P:P + 1], p("centre"), p("f_bv"), start=True, stop=True).then_inc(sem["setup_pe"], 1)

            def mix(step, j):
                if step == 2:
                    pe.wait_ge(sem["gate_ready"], j)
                    pe.wait_ge(sem["value_ready"], 3 * j)
                    pe.wait_ge(sem["x_mixed_ready"], j + 1)
                    mm(mix0[:, :], p("lora_a", 0, P), x_mixed[:, :], start=True, stop=True)
                    mm(mix1[0:RANK, :], p("lora_a", P), x_mixed[:, :], start=True, stop=True).then_inc(sem["lora_ps"], 1)
                if 3 <= step <= 7:
                    f = step - 3
                    ps = (mix0, mix1)[f % 2]
                    if f == 0:
                        pe.wait_ge(sem["lora_ready"], 2 * j + 2)
                    if f >= 2:
                        pe.wait_ge(sem["mixed_part"], MIXES * j + f - 1)
                    if f < 4:
                        lhs, rhs = p("lora_b")[f * RANK:(f + 1) * RANK], lora[f * RANK:(f + 1) * RANK, :]
                    else:
                        lhs, rhs = p("lora_b4", parts=RANK), lora4[:, :]
                    mm(ps[:, :], lhs, rhs, start=True, stop=True).then_inc(sem["miu_ps"], 1)
                if step == 8:
                    pe.wait_ge(sem["mixed_part"], MIXES * j + 5)
                    pe.wait_ge(sem["mixed_ready"], MIXES * j + 1)
                    mm(mix0[0:TD, :], p("td_a"), mixed[:, 0, :], start=True, stop=True).then_inc(sem["td_ps"], 1)
                if step == 9:
                    pe.wait_ge(sem["td_ready"], j + 1)
                    mm(mix0[:, :], p("td_b", parts=TD), td_hid[:, :], start=True, stop=True).then_inc(sem["w_ps"], 1)
                    pe.wait_ge(sem["mixed_ready"], MIXES * j + 2)
                    mm(mix1[:, :], p("wk"), mixed[:, 1, :], start=True, stop=True).then_inc(sem["k_ps"], 1)
                if step == 11:
                    pe.wait_ge(sem["exp_w_ready"], j + 1)
                    pe.wait_ge(sem["mixed_ready"], MIXES * j + 4)
                    mm(mix0[:, :], p("wr"), mixed[:, 3, :], start=True, stop=True).then_inc(sem["r_ps"], 1)
                if step == 13:
                    pe.wait_ge(sem["key_ready"], j + 1)
                    for c in range(SUB):
                        last = mm(mix1[:, c * P:(c + 1) * P], mixed[:, 2, c * P:(c + 1) * P], p("wv"), start=True, stop=True)
                    last.then_inc(sem["v_ps"], 1)
                if step == 16:
                    pe.wait_ge(sem["recep_ready"], 2 * j + 2)
                    pe.wait_ge(sem["mixed_ready"], MIXES * j + 5)
                    mm(mix0[:, :], p("wg"), mixed[:, 4, :], start=True, stop=True).then_inc(sem["g_ps"], 1)

            def wkv(step, j):
                if step <= LEVELS:
                    right = recep_u if step == 0 else recep
                    if step == 0:
                        pe.wait_ge(sem["key_ready"], j + 1)
                        pe.wait_ge(sem["recep_ready"], 2 * j + 2)
                        pe.wait_ge(sem["x1_ready"], j)
                    elif step == 1:
                        pe.wait_ge(sem["att_copied"], (LEVELS + 1) * j + 1)
                    else:
                        pe.wait_ge(sem["att_copied"], (LEVELS + 1) * j + step)
                        pe.wait_ge(sem["level_scaled"], (LEVELS + 1) * j + step - 1)
                    pe.sem_inc(sem["passed"], 1)
                    for c in range(SUB):
                        for h in range(HEADS):
                            for q in range(2):
                                tok = slice(c * P + q * 64, c * P + q * 64 + 64)
                                last = mm(by_head[q * 64:q * 64 + 64, h, c, :], key[h * 64:h * 64 + 64, tok],
                                          right[h * 64:h * 64 + 64, tok], start=True, stop=True)
                    last.then_inc(sem["level_ps"], 1)
                if step == 7:
                    pe.wait_ge(sem["att_copied"], (LEVELS + 1) * (j + 1))
                    pe.wait_ge(sem["level_scaled"], (LEVELS + 1) * j + LEVELS)
                    pe.sem_inc(sem["passed"], 1)
                    for c in range(SUB):
                        for h in range(HEADS):
                            last = mm(by_head[0:64, h, c, :], key[h * 64:h * 64 + 64, c * P:c * P + 64],
                                      recep[h * 64:h * 64 + 64, c * P + 64:c * P + P], start=True, stop=True)
                    last.then_inc(sem["off_ps"], 1)
                if step == 8:
                    pe.wait_ge(sem["off_ready"], j + 1)
                    pe.wait_ge(sem["level_scaled"], (LEVELS + 1) * (j + 1))
                    for c in range(SUB - 1):
                        last = pe.transpose(wkv0[:, c * P:(c + 1) * P], key[:, c * P:(c + 1) * P], p("ident"))
                    last.then_inc(sem["key_t_ps"], 1)
                    pe.wait_ge(sem["value_ready"], 3 * j + 3)
                    for c in range(SUB):
                        for h in range(HEADS):
                            lane = slice(h * 64, h * 64 + 64)
                            first, second = slice(c * P, c * P + 64), slice(c * P + 64, c * P + P)
                            mm(wkv1[lane, first], value_lo[:, c, lane], att[:, h, c, :], start=(c == 0), stop=False, skip_group_check=True)
                            mm(wkv1[lane, second], value_hi[:, c, lane], att[:, h, c, :], start=False, stop=False, skip_group_check=True)
                            last = mm(wkv1[lane, second], value_lo[:, c, lane], att_off[:, h, c, :], start=False, stop=(c == 0),
                                      skip_group_check=True)
                    last.then_inc(sem["intra_ps"], 1)
                if step == 9:
                    pe.wait_ge(sem["key_rows_ready"], j + 1)
                    for c in range(SUB - 1):
                        last = mm(wkv0[:, c * P:(c + 1) * P], key_rows[:, c, :], value[:, c, :], start=True, stop=True)
                    last.then_inc(sem["kv_ps"], 1)
                if step == 10:
                    pe.wait_ge(sem["state_ready"], j + 1)
                    for c in range(1, SUB):
                        last = mm(wkv1[:, c * P:(c + 1) * P], state[:, c - 1, :], recep[:, c * P:(c + 1) * P],
                                  start=False, stop=True, skip_group_check=True)
                    last.then_inc(sem["y_ps"], 1)
                if step == 11:
                    pe.wait_ge(sem["y_ready"], j + 1)
                    mm(wkv0[:, :], p("group_centre"), y_sb[:, :], start=True, stop=True).then_inc(sem["gn_cen_ps"], 1)
                if step == 12:
                    pe.wait_ge(sem["gn_sq_ready"], j + 1)
                    columns(wkv1, HEADS, wkv_sq, p("group_var")).then_inc(sem["gn_var_ps"], 1)
                if step == 13:
                    pe.wait_ge(sem["gn_cen_ready"], j + 1)
                    pe.wait_ge(sem["gn_rstd_ready"], j + 1)
                    broadcast(wkv0, gn_rstd, HEADS).then_inc(sem["gn_bc_ps"], 1)
                if step == 14:
                    pe.wait_ge(sem["x_res_split"], 2 * j + 2)
                    pe.wait_ge(sem["gated_ready"], j + 1)
                    mm(wkv0[:, :], centre_exact, x_res_high[:, :], start=True, stop=False)
                    mm(wkv0[:, :], centre_exact, x_res_low[:, :], start=False, stop=False)
                    mm(wkv0[:, :], c_wo, gated[:, :], start=False, stop=True).then_inc(sem["o_ps"], 1)
                if step == 15:
                    pe.wait_ge(sem["ln1_sq_ready"], j + 1)
                    columns(wkv1, 1, wkv_sq, p("mean_col", 0, 1)).then_inc(sem["ln1_var_ps"], 1)
                if step == 16:
                    pe.wait_ge(sem["ln1_cen_ready"], j + 1)
                    pe.wait_ge(sem["ln1_rstd_ready"], j + 1)
                    broadcast(wkv0, ln1_rstd, 1).then_inc(sem["ln1_bc_ps"], 1)

            def ffn(step, j):
                if step == 0:
                    pe.wait_ge(sem["x2_ready"], j)
                    pe.wait_ge(sem["x1_ready"], j + 1)
                    mm(ffn0[:, :], p("fv"), x1[:, :], start=True, stop=True).then_inc(sem["val_ps"], 1)
                if step == 1:
                    pe.wait_ge(sem["val_ready"], j + 1)
                    w = E0 * (1 + PROTO)
                    columns(ffn1, w, val, p("f_router")).then_inc(sem["router_ps"], 1)
                if step in (3, 5):
                    n = (step - 3) // 2
                    if n == 1:
                        pe.wait_ge(sem["h_read"], 4 * j + 2)
                    mm(ffn0[:, :], p("f_w1", n * P, (n + 1) * P), val[:, :], start=True, stop=True).then_inc(sem["h_ps"], 1)
                if step == 9:
                    pe.wait_ge(sem["expert_w_ready"], 3 * j + 3)
                    for c in range(SUB):
                        last = pe.transpose(ffn1[0:3 * E0, c * P:(c + 1) * P], expert_w3[:, c, :], p("ident"))
                    last.then_inc(sem["wt_ps"], 1)
                if step == 10:
                    pe.wait_ge(sem["h_read"], 4 * j + 4)
                    pe.wait_ge(sem["wt_ready"], j + 1)
                    for n, ps in enumerate((ffn0, ffn1)):
                        mm(ps[:, :], spread_exact[n], expert_wt[:, :],
                           start=True, stop=True).then_inc(sem["spread_ps"], 1)
                if step == 11:
                    pe.wait_ge(sem["hid_ready"], 2 * j + 2)
                    mm(ffn0[:, :], c_fv, x1[:, :], start=True, stop=False)
                    mm(ffn0[:, :], c_b2[:, :], expert_wt[:, :], start=False, stop=False)
                    mm(ffn0[:, :], c_w2[0], hid[:, 0, :], start=False, stop=False)
                    mm(ffn0[:, :], c_w2[1], hid[:, 1, :], start=False, stop=True).then_inc(sem["delta_ps"], 1)
                if step == 12:
                    pe.wait_ge(sem["ln2_sq_ready"], j + 1)
                    columns(ffn1, 1, ffn_sq, p("mean_col", 0, 1)).then_inc(sem["ln2_var_ps"], 1)
                if step == 13:
                    pe.wait_ge(sem["ln2_cen_ready"], j + 1)
                    pe.wait_ge(sem["ln2_rstd_ready"], j + 1)
                    broadcast(ffn0, ln2_rstd, 1).then_inc(sem["ln2_bc_ps"], 1)

            def gru(step, j):
                if step == 0:
                    pe.wait_ge(sem["rows_ready"], 3 * j)
                    pe.wait_ge(sem["x2_ready"], j + 1)
                    mm(gru0[:, :], p("wz"), x2[:, :], start=True, stop=True).then_inc(sem["z_ps"], 1)
                if step == 1:
                    pe.wait_ge(sem["slots_ready"], j)
                    mm(gru1[:, :], p("wh"), x2[:, :], start=True, stop=True).then_inc(sem["t_ps"], 1)
                if step == 4:
                    pe.wait_ge(sem["z_read"], j + 1)
                    pe.wait_ge(sem["hidden_ready"], j + 1)
                    mm(gru0[:, :], p("centre"), x2[:, :], start=True, stop=False)
                    mm(gru0[:, :], c_quarter, hidden[:, :], start=False, stop=True).then_inc(sem["g_out_ps"], 1)
                if step == 5:
                    pe.wait_ge(sem["t_read"], 2 * j + 2)
                    pe.wait_ge(sem["ln3_sq_ready"], j + 1)
                    columns(gru1, 1, gru_sq, p("mean_col", 0, 1)).then_inc(sem["ln3_var_ps"], 1)
                if step == 6:
                    pe.wait_ge(sem["ln3_cen_ready"], j + 1)
                    pe.wait_ge(sem["ln3_rstd_ready"], j + 1)
                    broadcast(gru0, ln3_rstd, 1).then_inc(sem["ln3_bc_ps"], 1)
                if step == 8:
                    pe.wait_ge(sem["x3_ready"], j + 1)
                    columns(gru1, E1, x3, p("e_router")).then_inc(sem["logits_ps"], 1)
                    for c in range(SUB):
                        last = pe.transpose(gru0[:, c * P:(c + 1) * P], x3[:, c * P:(c + 1) * P], p("ident"))
                    last.then_inc(sem["rows_ps"], 1)
                if step == 12:
                    pe.wait_ge(sem["chosen_ready"], j + 1)
                    mm(gru1[:, 0:SUB * E1], p("upper"), chosen[:, :, :].rearrange("p c e -> p (c e)"), start=True, stop=False)
                    mm(gru1[:, 0:SUB * E1], p("ones"), seen[:, 0:SUB, :].rearrange("p c e -> p (c e)"),
                       start=False, stop=True).then_inc(sem["rank_ps"], 1)

            pipeline(pe, (mix, wkv, ffn, gru), PE_ORDER)
            experts_pe(pe)

        @block.scalar
        def _(act):
            def f(out, in_, func, **kw):
                return nc.scalar.activation(out, in_, func, **kw)

            act.wait_ge(sem["params_in"], 16)
            f(sig_alpha, p("alpha"), ACT.Tanh, scale=0.5).then_inc(sem["alpha_tanh"], 1)

            def mix(step, j):
                if step == 2:
                    act.wait_ge(sem["lora_ps"], j + 1)
                    f(lora[:, :], mix0[:, :], ACT.Tanh).then_inc(sem["lora_ready"], 1)
                    f(lora4[:, :], mix1[0:RANK, :], ACT.Tanh).then_inc(sem["lora_ready"], 1)
                if step == 8:
                    act.wait_ge(sem["td_ps"], j + 1)
                    f(td_hid[:, :], mix0[0:TD, :], ACT.Tanh).then_inc(sem["td_ready"], 1)
                if step == 10:
                    act.wait_ge(sem["w_ps"], j + 1)
                    f(exp_w[:, :], mix0[:, :], ACT.Exp, bias=p("td_miu")).then_inc(sem["exp_w_ready"], 1)
                    act.wait_ge(sem["exp_w_ready"], j + 1)
                    act.wait_ge(sem["level_scaled"], (LEVELS + 1) * j)
                    f(decay[:, :], exp_w[:, :], ACT.Exp, scale=-1.0).then_inc(sem["decay_ready"], 1)
                if step == 12:
                    act.wait_ge(sem["k_ps"], j + 1)
                    act.wait_ge(sem["y_ps"], j)
                    f(key[:, :], mix1[:, :], ACT.Copy).then_inc(sem["key_ready"], 1)
                    act.wait_ge(sem["r_ps"], j + 1)
                    f(recep[:, :], mix0[:, :], ACT.Copy).then_inc(sem["recep_ready"], 1)
                    f(recep_u[:, :], mix0[:, :], ACT.Identity, scale=p("bonus")).then_inc(sem["recep_ready"], 1)
                if step == 14:
                    act.wait_ge(sem["v_ps"], j + 1)
                    for dst, lane in ((value, slice(0, P)), (value_lo, slice(0, 64)), (value_hi, slice(64, P))):
                        f(dst[lane, :, :].rearrange("p c n -> p (c n)"), mix1[lane, :], ACT.Copy).then_inc(sem["value_ready"], 1)
                if step == 16:
                    act.wait_ge(sem["g_ps"], j + 1)
                    f(tanh_g[:, :], mix0[:, :], ACT.Tanh, scale=0.5).then_inc(sem["tanh_g_ready"], 1)

            def wkv(step, j):
                if step == 7:
                    act.wait_ge(sem["off_ps"], j + 1)
                    f(att_off[0:64, :, :, :], by_head[0:64], ACT.Copy).then_inc(sem["off_ready"], 1)
                if step == 8:
                    act.wait_ge(sem["key_t_ps"], j + 1)
                    f(key_rows[:, :, :].rearrange("p c n -> p (c n)"), wkv0[:, 0:(SUB - 1) * P], ACT.Copy).then_inc(sem["key_rows_ready"], 1)
                if step == 10:
                    act.wait_ge(sem["y_ps"], j + 1)
                    f(y_sb[:, :], wkv1[:, :], ACT.Copy).then_inc(sem["y_ready"], 1)
                if step == 11:
                    act.wait_ge(sem["gn_cen_ps"], j + 1)
                    f(wkv_sq[:, :], wkv0[:, :], ACT.Square).then_inc(sem["gn_sq_ready"], 1)
                    f(wkv_cen[:, :], wkv0[:, :], ACT.Copy).then_inc(sem["gn_cen_ready"], 1)
                if step == 14:
                    act.wait_ge(sem["o_ps"], j + 1)
                    f(wkv_sq[:, :], wkv0[:, :], ACT.Square).then_inc(sem["ln1_sq_ready"], 1)
                    f(wkv_cen[:, :], wkv0[:, :], ACT.Copy).then_inc(sem["ln1_cen_ready"], 1)

            def ffn(step, j):
                if step == 0:
                    act.wait_ge(sem["val_ps"], j + 1)
                    f(val[:, :], ffn0[:, :], ACT.Identity, bias=p("f_bv")).then_inc(sem["val_ready"], 1)
                if step == 1:
                    act.wait_ge(sem["router_step"], ROUTER_STEPS * j + 1)
                    routed = ffn1[:, 0:SUB * E0 * (1 + PROTO)].rearrange("p (c w) -> p c w", c=SUB)
                    f(proto_sq[:, :, :], routed[:, :, E0:], ACT.Square).then_inc(sem["proto_sq_ready"], 1)
                if step in (4, 6):
                    n = (step - 4) // 2
                    act.wait_ge(sem["h_ps"], 2 * j + n + 1)
                    f(tanh_h[:, n, :], ffn0[:, :], ACT.Tanh, scale=0.5, bias=half_b1[:, n:n + 1]).then_inc(sem["h_read"], 1)
                    f(half_h[:, n, :], ffn0[:, :], ACT.Identity, scale=0.5, bias=half_b1[:, n:n + 1]).then_inc(sem["h_read"], 1)
                if step == 8:
                    act.wait_ge(sem["ffn_gap_ready"], j + 1)
                    f(ffn_top.ratio[:, :], ffn_top.gap[:, :], ACT.Exp).then_inc(sem["ffn_ratio_ready"], 1)
                if step == 9:
                    act.wait_ge(sem["wt_ps"], j + 1)
                    f(expert_wt[:, :], ffn1[0:3 * E0, :], ACT.Copy).then_inc(sem["wt_ready"], 1)
                if step == 11:
                    act.wait_ge(sem["delta_ps"], j + 1)
                    f(ffn_sq[:, :], ffn0[:, :], ACT.Square, bias=c_bv).then_inc(sem["ln2_sq_ready"], 1)
                    f(ffn_cen[:, :], ffn0[:, :], ACT.Identity, bias=c_bv).then_inc(sem["ln2_cen_ready"], 1)

            def gru(step, j):
                if step == 0:
                    act.wait_ge(sem["z_ps"], j + 1)
                    f(tanh_z[:, :], gru0[:, :], ACT.Tanh, scale=0.5, bias=half_bz).then_inc(sem["z_read"], 1)
                    act.wait_ge(sem["t_ps"], j + 1)
                    f(tanh_t[:, :], gru1[:, :], ACT.Tanh, scale=0.5, bias=half_bh).then_inc(sem["t_read"], 1)
                    f(lin_t[:, :], gru1[:, :], ACT.Identity, scale=2.0, bias=double_bh).then_inc(sem["t_read"], 1)
                if step == 4:
                    act.wait_ge(sem["g_out_ps"], j + 1)
                    f(gru_sq[:, :], gru0[:, :], ACT.Square).then_inc(sem["ln3_sq_ready"], 1)
                    f(gru_cen[:, :], gru0[:, :], ACT.Copy).then_inc(sem["ln3_cen_ready"], 1)
                if step == 8:
                    act.wait_ge(sem["rows_ps"], j + 1)
                    act.wait_ge(sem["scattered"], 16 * 2 * SUB * j)
                    turned = gru0[:, :].rearrange("p (c n) -> p c n", c=SUB)
                    for n in range(2):
                        f(x3_rows[:, n, :, 0:P], turned, ACT.Copy).then_inc(sem["rows_ready"], 1)
                    kept = x3_kept[:, j, :, :] if isinstance(j, int) else x3_kept[:, bass.ds(j, 1), :, :].rearrange("p o c n -> p (o c) n")
                    f(kept, turned, ACT.Copy).then_inc(sem["rows_ready"], 1)
                if step == 11:
                    act.wait_ge(sem["gru_gap_ready"], j + 1)
                    f(gru_top.ratio[:, :], gru_top.gap[:, :], ACT.Exp).then_inc(sem["gru_ratio_ready"], 1)

            act.wait_ge(sem["setup_done"], 1)
            pipeline(act, (mix, wkv, ffn, gru))
            experts_act(act)
            last_act(act)

        def top2_pick(link, s, top):
            desc = p("descend").rearrange("p (c e) -> p c e", c=SUB)
            for n, src in ((0, s), (1, top.rest[:, :, :])):
                link(nc.vector.tensor_reduce(top.best[:, n, :], src, AX_X, ALU.max))
                link(nc.vector.tensor_tensor(top.equal[:, :, :], src, top.best[:, n, :].unsqueeze(2).to_broadcast([P, SUB, E0]), ALU.is_equal))
                link(nc.vector.tensor_tensor(top.equal[:, :, :], top.equal[:, :, :], desc, ALU.mult))
                link(nc.vector.tensor_reduce(top.rank[:, :], top.equal[:, :, :], AX_X, ALU.max))
                link(nc.vector.tensor_tensor(top.hot[:, n, :, :], desc, top.rank[:, :].unsqueeze(2).to_broadcast([P, SUB, E0]), ALU.is_equal))
                if n == 0:
                    link(nc.vector.scalar_tensor_tensor(top.rest[:, :, :], top.hot[:, 0, :, :], -BIG, s, ALU.mult, ALU.add))

        @block.vector
        def _(dve):
            v = nc.vector
            tt, ts, stt = v.tensor_tensor, v.tensor_scalar, v.scalar_tensor_tensor

            def linker(signal, base):
                count = [0]

                def link(ins):
                    count[0] += 1
                    ins.then_inc(signal, 1)
                    dve.wait_ge(signal, base + count[0])
                return link, count

            setup, _ = linker(sem["setup_dve"], 0)
            v.memset(no_output[:, :], 0.0).then_inc(sem["cleared"], 1)
            setup(v.memset(empty_slot[:, :], 0.0))
            v.memset(empty_slot[:, P:P + 1], float(B * P * 2 * SUB)).then_inc(sem["cleared"], 1)
            setup(v.memset(x_in[:, 0:1], 0.0))
            setup(v.memset(att[:, :, :, :], 0.0))
            setup(v.memset(att_off[:, :, :, :], 0.0))
            setup(v.memset(value_lo[:, :, :], 0.0))
            setup(v.memset(value_hi[:, :, :], 0.0))
            setup(v.memset(state[:, :, :], 0.0))
            setup(v.memset(seen[:, :, :], 0.0))
            dve.wait_ge(sem["params_in"], 16)
            setup(v.tensor_copy(dest[:, :, :].rearrange("p n c -> p (n c)"), p("dest_base")))
            setup(v.memset(powers[:, 0, :], -0.5))
            setup(v.memset(powers[:, 1, :], 0.5))
            dve.wait_ge(sem["params_in"], 16)
            setup(ts(half_beta, p("gn_beta"), 0.5, None, ALU.mult))
            setup(ts(half_b1, p("f_b1"), 0.5, None, ALU.mult))
            setup(ts(half_bz, p("b_z"), 0.5, None, ALU.mult))
            setup(ts(half_bh, p("b_h"), 0.5, None, ALU.mult))
            setup(ts(double_bh, p("b_h"), 2.0, None, ALU.mult))
            setup(ts(c_quarter, p("centre"), 0.25, None, ALU.mult))
            dve.wait_ge(sem["alpha_tanh"], 1)
            setup(ts(small[:, 8:9], sig_alpha, 0.5, 0.5, ALU.mult, ALU.add))
            setup(ts(router_scale[:, 0, :], p("f_gr"), float(E0) ** 0.5, None, ALU.mult))
            setup(ts(router_scale[:, 1, :], p("f_gc"), small[:, 8:9], float(E0) ** 0.5, ALU.mult, ALU.mult))
            setup(stt(router_shift[:, :], p("f_bc"), small[:, 8:9], p("f_br"), ALU.mult, ALU.add))
            dve.wait_ge(sem["setup_pe"], 1)
            setup(v.tensor_copy(folded[:, 0:4 * P], mix0[:, :]))
            setup(v.tensor_copy(c_b2_high[:, :], mix1[0:3 * E0, 0:P]))
            setup(stt(c_b2[:, :], c_b2_high[:, :], p("low_rows", parts=3 * E0), mix1[0:3 * E0, 0:P], ALU.mult, ALU.add))
            setup(v.tensor_copy(exact[:, :], par[:, 0:3 * P]))
            setup(v.tensor_copy(c_bv, mix1[:, P:P + 1]))
            dve.wait_ge(sem["masks_in"], 16)
            v.memset(small[:, 9:10], 0.0).then_inc(sem["setup_done"], 1)

            def mix(step, j):
                if step == 0:
                    dve.wait_ge(sem["x_in_loaded"], 16 * (j + 1))
                    tt(dx[:, :], x_in[:, 0:T], x_in[:, 1:T + 1], ALU.subtract).then_inc(sem["dx_ready"], 1)
                if step == 1:
                    dve.wait_ge(sem["dx_ready"], j + 1)
                    stt(x_mixed[:, :], dx[:, :], p("miu_x"), x_in[:, 1:T + 1], ALU.mult, ALU.add).then_inc(sem["x_mixed_ready"], 1)
                if 3 <= step <= 7:
                    f = step - 3
                    dve.wait_ge(sem["miu_ps"], MIXES * j + f + 1)
                    if f == 0:
                        dve.wait_ge(sem["g_ps"], j)
                    stt(mixed[:, f, :], (mix0, mix1)[f % 2][:, :], p("lam", f, f + 1), dx[:, :], ALU.add, ALU.mult).then_inc(sem["mixed_part"], 1)
                if step == 16:
                    dve.wait_ge(sem["tanh_g_ready"], j + 1)
                    dve.wait_ge(sem["gated_ready"], j)
                    stt(gate[:, :], tanh_g[:, :], 1.0, mix0[:, :], ALU.add, ALU.mult).then_inc(sem["gate_ready"], 1)

            def scale_level(j, level):
                b = 1 << level
                n = T // b
                off = 0 if level <= 1 else T - (T >> (level - 1))
                tot = decay[:, :] if level == 0 else total[:, off:off + n]
                nxt_off = 0 if level == 0 else T - (T >> level)
                halves = tot.rearrange("p (n two) -> p n two", two=2)
                left = halves[:, :, 0:1].to_broadcast([P, n // 2, b]) if b > 1 else halves[:, :, 0:1]
                right = halves[:, :, 1:2].to_broadcast([P, n // 2, b]) if b > 1 else halves[:, :, 1:2]
                r = recep[:, :].rearrange("p (n two b) -> p n two b", two=2, b=b)[:, :, 1, :]
                k = key[:, :].rearrange("p (n two b) -> p n two b", two=2, b=b)[:, :, 0, :]
                if level == 0:
                    dve.wait_ge(sem["decay_ready"], j + 1)
                    dve.wait_ge(sem["level_ps"], (LEVELS + 1) * j + 2)
                elif level < LEVELS:
                    dve.wait_ge(sem["level_ps"], (LEVELS + 1) * j + level + 2)
                    dve.wait_ge(sem["level_scaled"], (LEVELS + 1) * j + level)
                else:
                    dve.wait_ge(sem["off_ps"], j + 1)
                    dve.wait_ge(sem["level_scaled"], (LEVELS + 1) * j + level)
                tt(total[:, nxt_off:nxt_off + n // 2], halves[:, :, 0], halves[:, :, 1], ALU.mult)
                tt(r, r, left, ALU.mult)
                tt(k, k, right, ALU.mult).then_inc(sem["level_scaled"], 1)

            def wkv(step, j):
                if step <= LEVELS:
                    dve.wait_ge(sem["level_ps"], (LEVELS + 1) * j + step + 1)
                    if step == 0:
                        dve.wait_ge(sem["intra_ps"], j)
                    else:
                        dve.wait_ge(sem["att_copied"], (LEVELS + 1) * j + step)
                    dve.sem_inc(sem["passed"], 1)
                    v.copy_predicated(att[:, :, :, :], mask[:, step, :].unsqueeze(1).unsqueeze(1).to_broadcast([P, HEADS, SUB, 64]),
                                      by_head).then_inc(sem["att_copied"], 1)
                    if step >= 1:
                        scale_level(j, step - 1)
                if step == 7:
                    scale_level(j, LEVELS)
                if step == 9:
                    dve.wait_ge(sem["kv_ps"], j + 1)
                    tot_off = T - (T >> LEVELS)
                    for c in range(SUB - 1):
                        if c:
                            dve.wait_ge(sem["state_step"], 2 * (SUB - 2) * j + 2 * c)
                        for h in range(HEADS):
                            lane = slice(h * 64, h * 64 + 64)
                            kv = wkv0[lane, c * P + h * 64:c * P + h * 64 + 64]
                            if c == 0:
                                ins = v.tensor_copy(state[lane, 0, lane], kv)
                            else:
                                ins = stt(state[lane, c, lane], state[lane, c - 1, lane], total[lane, tot_off + c:tot_off + c + 1],
                                          kv, ALU.mult, ALU.add)
                            if c < SUB - 2:
                                ins.then_inc(sem["state_step"], 1)
                            elif h == HEADS - 1:
                                ins.then_inc(sem["state_ready"], 1)
                if step == 12:
                    dve.wait_ge(sem["gn_var_ps"], j + 1)
                    ts(gn_var[:, :], wkv1[:, 0:SUB * HEADS], 4 * EPS * HEADS, None, ALU.add).then_inc(sem["gn_var_ready"], 1)
                if step == 13:
                    dve.wait_ge(sem["gn_bc_ps"], j + 1)
                    tt(gated[:, :], wkv_cen[:, :], wkv0[:, :], ALU.mult).then_inc(sem["gated_step"], 1)
                    dve.wait_ge(sem["gated_step"], 2 * j + 1)
                    dve.wait_ge(sem["gate_ready"], j + 1)
                    ts(gated[:, :], gated[:, :], p("gn_gamma"), half_beta, ALU.mult, ALU.add).then_inc(sem["gated_step"], 1)
                    dve.wait_ge(sem["gated_step"], 2 * j + 2)
                    tt(gated[:, :], gated[:, :], gate[:, :], ALU.mult).then_inc(sem["gated_ready"], 1)
                if step == 15:
                    dve.wait_ge(sem["ln1_var_ps"], j + 1)
                    ts(ln1_var[:, :], wkv1[:, 0:SUB], EPS, None, ALU.add).then_inc(sem["ln1_var_ready"], 1)
                if step == 16:
                    dve.wait_ge(sem["ln1_bc_ps"], j + 1)
                    dve.wait_ge(sem["delta_ps"], j)
                    tt(x1[:, :], wkv_cen[:, :], wkv0[:, :], ALU.mult).then_inc(sem["x1_ready"], 1)

            def ffn(step, j):
                if step == 1:
                    dve.wait_ge(sem["router_ps"], j + 1)
                    routed = ffn1[:, 0:SUB * E0 * (1 + PROTO)].rearrange("p (c w) -> p c w", c=SUB)
                    bg = p("f_bg").unsqueeze(1).to_broadcast([P, SUB, E0])
                    tt(rc[:, 0, :, :], routed[:, :, 0:E0], bg, ALU.add).then_inc(sem["router_step"], 1)
                if step == 2:
                    link, _ = linker(sem["router_step"], j * ROUTER_STEPS + 1)
                    dve.wait_ge(sem["proto_sq_ready"], j + 1)
                    link(v.tensor_reduce(norm_sq[:, :, :], proto_sq[:, :, :].rearrange("p c (e q) -> p c e q", q=PROTO), AX_X, ALU.add))
                    ts(rc_sq[:, 1, :, :], norm_sq[:, :, :], 1.0 / PROTO, None, ALU.mult).then_inc(sem["norm_sq_ready"], 1)
                if step == 4:
                    link, _ = linker(sem["router_step"], j * ROUTER_STEPS + 2)
                    dve.wait_ge(sem["norm_ready"], j + 1)
                    link(v.tensor_reduce(rc_sum[:, :], rc[:, :, :, :].rearrange("p k c e -> p (k c) e"), AX_X, ALU.add))
                    mean = rc_sum[:, :].unsqueeze(2).to_broadcast([P, 2 * SUB, E0])
                    flat = rc[:, :, :, :].rearrange("p k c e -> p (k c) e")
                    link(stt(rc_cen[:, :, :, :].rearrange("p k c e -> p (k c) e"), mean, -1.0 / E0, flat, ALU.mult, ALU.add))
                    link(tt(rc_sq[:, :, :, :], rc_cen[:, :, :, :], rc_cen[:, :, :, :], ALU.mult))
                    link(v.tensor_reduce(rc_sum[:, :], rc_sq[:, :, :, :].rearrange("p k c e -> p (k c) e"), AX_X, ALU.add))
                    ts(rc_sum[:, :], rc_sum[:, :], E0 * EPS, None, ALU.add).then_inc(sem["rc_sq_ready"], 1)
                if step == 6:
                    link, _ = linker(sem["router_step"], j * ROUTER_STEPS + 6)
                    dve.wait_ge(sem["rc_rstd_ready"], j + 1)
                    rstd = rc_rstd[:, :].unsqueeze(2).to_broadcast([P, 2 * SUB, E0])
                    link(tt(rc_norm[:, :, :, :].rearrange("p k c e -> p (k c) e"), rc_cen[:, :, :, :].rearrange("p k c e -> p (k c) e"), rstd, ALU.mult))
                    for k in range(2):
                        g = router_scale[:, k:k + 1, :].to_broadcast([P, SUB, E0])
                        link(tt(rc_norm[:, k, :, :], rc_norm[:, k, :, :], g, ALU.mult))
                    link(tt(rc_norm[:, 0, :, :], rc_norm[:, 0, :, :], rc_norm[:, 1, :, :], ALU.add))
                    link(tt(rc_norm[:, 0, :, :], rc_norm[:, 0, :, :], router_shift[:, :].unsqueeze(1).to_broadcast([P, SUB, E0]), ALU.add))
                if step == 7:
                    link, _ = linker(sem["router_step"], j * ROUTER_STEPS + 11)
                    top2_pick(link, rc_norm[:, 0, :, :], ffn_top)
                    tt(ffn_top.gap[:, :], ffn_top.best[:, 1, :], ffn_top.best[:, 0, :], ALU.subtract).then_inc(sem["ffn_gap_ready"], 1)
                if step == 8:
                    link, _ = linker(sem["router_step"], j * ROUTER_STEPS + 22)
                    dve.wait_ge(sem["ffn_ratio_ready"], j + 1)
                    shares(link, ffn_top)
                    for n in range(2):
                        w = ffn_top.share[:, :, n:n + 1].to_broadcast([P, SUB, E0])
                        link(tt(ffn_top.hot[:, n, :, :], ffn_top.hot[:, n, :, :], w, ALU.mult))
                    part, _ = linker(sem["expert_w_ready"], 3 * j)
                    part(tt(expert_w[:, :, :], ffn_top.hot[:, 0, :, :], ffn_top.hot[:, 1, :, :], ALU.add))
                    part(v.tensor_copy(expert_w_high[:, :, :], expert_w[:, :, :]))
                    v.tensor_copy(expert_w3[:, :, 0:E0], expert_w_high[:, :, :])
                    v.tensor_copy(expert_w3[:, :, 2 * E0:3 * E0], expert_w_high[:, :, :])
                    tt(expert_w3[:, :, E0:2 * E0], expert_w[:, :, :], expert_w_high[:, :, :], ALU.subtract).then_inc(sem["expert_w_ready"], 1)
                if step in (4, 6):
                    n = (step - 4) // 2
                    dve.wait_ge(sem["h_read"], 4 * j + 2 * n + 2)
                    stt(tanh_h[:, n, :], tanh_h[:, n, :], 1.0, half_h[:, n, :], ALU.add, ALU.mult).then_inc(sem["silu_ready"], 1)
                if step == 10:
                    dve.wait_ge(sem["silu_ready"], 2 * j + 2)
                    for n, ps in enumerate((ffn0, ffn1)):
                        dve.wait_ge(sem["spread_ps"], 2 * j + n + 1)
                        tt(hid[:, n, :], tanh_h[:, n, :], ps[:, :], ALU.mult).then_inc(sem["hid_ready"], 1)
                if step == 12:
                    dve.wait_ge(sem["ln2_var_ps"], j + 1)
                    ts(ln2_var[:, :], ffn1[:, 0:SUB], EPS, None, ALU.add).then_inc(sem["ln2_var_ready"], 1)
                if step == 13:
                    dve.wait_ge(sem["ln2_bc_ps"], j + 1)
                    dve.wait_ge(sem["g_out_ps"], j)
                    tt(x2[:, :], ffn_cen[:, :], ffn0[:, :], ALU.mult).then_inc(sem["x2_ready"], 1)

            def shares(link, top):
                link(ts(top.den[:, :], top.ratio[:, :], 1.0, None, ALU.add))
                link(v.reciprocal(top.share[:, :, 0], top.den[:, :]))
                link(tt(top.share[:, :, 1], top.ratio[:, :], top.share[:, :, 0], ALU.mult))

            def gru(step, j):
                if step == 1:
                    link, _ = linker(sem["gru_step"], 4 * j)
                    dve.wait_ge(sem["t_read"], 2 * j + 2)
                    dve.wait_ge(sem["z_read"], j + 1)
                    link(tt(lin_t[:, :], lin_t[:, :], tanh_t[:, :], ALU.max))
                    link(ts(keep_z[:, :], tanh_z[:, :], -0.5, 0.5, ALU.mult, ALU.add))
                if step == 2:
                    link, _ = linker(sem["gru_step"], 4 * j + 2)
                    link(ts(take_z[:, :], tanh_z[:, :], 1.0, None, ALU.add))
                    link(stt(take_z[:, :], lin_t[:, :], 1.0, take_z[:, :], ALU.add, ALU.mult))
                    v.tensor_tensor_scan(hidden[:, :], keep_z[:, :], take_z[:, :], 0.0, ALU.mult, ALU.add).then_inc(sem["hidden_ready"], 1)
                if step == 4:
                    dve.wait_ge(sem["ln3_var_ps"], j + 1)
                    ts(ln3_var[:, :], gru1[:, 0:SUB], EPS, None, ALU.add).then_inc(sem["ln3_var_ready"], 1)
                if step == 7:
                    dve.wait_ge(sem["ln3_bc_ps"], j + 1)
                    tt(x3[:, :], gru_cen[:, :], gru0[:, :], ALU.mult).then_inc(sem["x3_ready"], 1)
                if step == 10:
                    link, _ = linker(sem["route_step"], j * ROUTE_STEPS)
                    dve.wait_ge(sem["logits_ps"], j + 1)
                    br = p("e_br").unsqueeze(1).to_broadcast([P, SUB, E1])
                    link(tt(logits[:, :, :], gru1[:, 0:SUB * E1].rearrange("p (c e) -> p c e", c=SUB), br, ALU.add))
                    top2_pick(link, logits[:, :, :], gru_top)
                    tt(gru_top.gap[:, :], gru_top.best[:, 1, :], gru_top.best[:, 0, :], ALU.subtract).then_inc(sem["gru_gap_ready"], 1)
                    link(tt(chosen[:, :, :], gru_top.hot[:, 0, :, :], gru_top.hot[:, 1, :, :], ALU.add))
                    link(v.tensor_copy(seen[:, 0, :], seen[:, SUB, :]))
                    for c in range(SUB):
                        ins = tt(seen[:, c + 1, :], seen[:, c, :], chosen[:, c, :], ALU.add)
                        if c < SUB - 1:
                            link(ins)
                    ins.then_inc(sem["chosen_ready"], 1)
                if step == 16:
                    link, _ = linker(sem["route_step"], j * ROUTE_STEPS + 17)
                    dve.wait_ge(sem["gru_ratio_ready"], j + 1)
                    shares(link, gru_top)
                    dve.wait_ge(sem["rank_ps"], j + 1)
                    rank = gru1[:, 0:SUB * E1].rearrange("p (c e) -> p c e", c=SUB)
                    link(ts(over[:, :, :], rank, float(CAP), float(SLOTS), ALU.is_ge, ALU.mult))
                    link(tt(slot_of[:, :, :], rank, p("slot_base").rearrange("p (c e) -> p c e", c=SUB), ALU.add))
                    link(tt(slot_of[:, :, :], slot_of[:, :, :], over[:, :, :], ALU.max))
                    for n in range(2):
                        link(tt(pick_tmp[:, :, n, :], slot_of[:, :, :], gru_top.hot[:, n, :, :], ALU.mult))
                    link(v.tensor_reduce(slot_f[:, :, :], pick_tmp[:, :, :, :], AX_X, ALU.add))
                    dve.wait_ge(sem["scattered"], 16 * 2 * SUB * j)
                    link(v.tensor_copy(slot_scatter[:, :], slot_f[:, :, :].rearrange("p c n -> p (c n)")))
                    link(v.tensor_copy(x3_rows[:, :, :, P], dest[:, :, :]))
                    link(ts(dest[:, :, :], dest[:, :, :], float(P * 2 * SUB), None, ALU.add))
                    v.tensor_copy(x3_rows[:, :, :, P + 1], gru_top.share[:, :, :].rearrange("p c n -> p n c")).then_inc(sem["slots_ready"], 1)

            pipeline(dve, (mix, wkv, ffn, gru))
            experts_dve(dve)
            last_dve(dve)

        @block.gpsimd
        def _(pool):
            g = nc.gpsimd
            pool.wait_ge(sem["setup_done"], 1)

            def power(out, in_, which, n):
                return g.tensor_tensor(out, in_, powers[:, which, 0:n], ALU.pow)

            def mix(step, j):
                if 4 <= step <= 8:
                    f = step - 4
                    pool.wait_ge(sem["mixed_part"], MIXES * j + f + 1)
                    g.tensor_tensor(mixed[:, f, :], mixed[:, f, :], x_in[:, 1:T + 1], ALU.add).then_inc(sem["mixed_ready"], 1)

            def wkv(step, j):
                if step == 9:
                    pool.wait_ge(sem["x_res_loaded"], 16 * (j + 1))
                    pool.wait_ge(sem["o_ps"], j)
                    pool.sem_inc(sem["passed"], 1)
                    g.tensor_copy(x_res_high[:, :], x_res[:, :]).then_inc(sem["x_res_split"], 1)
                    pool.wait_ge(sem["x_res_split"], 2 * j + 1)
                    g.tensor_tensor(x_res_low[:, :], x_res[:, :], x_res_high[:, :], ALU.subtract).then_inc(sem["x_res_split"], 1)
                if step == 12:
                    pool.wait_ge(sem["gn_var_ready"], j + 1)
                    power(gn_rstd[:, :], gn_var[:, :], 0, SUB * HEADS).then_inc(sem["gn_rstd_ready"], 1)
                if step == 15:
                    pool.wait_ge(sem["ln1_var_ready"], j + 1)
                    power(ln1_rstd[:, :], ln1_var[:, :], 0, SUB).then_inc(sem["ln1_rstd_ready"], 1)

            def ffn(step, j):
                if step == 2:
                    pool.wait_ge(sem["norm_sq_ready"], j + 1)
                    power(rc[:, 1, :, :].rearrange("p c e -> p (c e)"), rc_sq[:, 1, :, :].rearrange("p c e -> p (c e)"), 1,
                          SUB * E0).then_inc(sem["norm_ready"], 1)
                if step == 5:
                    pool.wait_ge(sem["rc_sq_ready"], j + 1)
                    power(rc_rstd[:, :], rc_sum[:, :], 0, 2 * SUB).then_inc(sem["rc_rstd_ready"], 1)
                if step == 12:
                    pool.wait_ge(sem["ln2_var_ready"], j + 1)
                    power(ln2_rstd[:, :], ln2_var[:, :], 0, SUB).then_inc(sem["ln2_rstd_ready"], 1)

            def gru(step, j):
                if step == 4:
                    pool.wait_ge(sem["ln3_var_ready"], j + 1)
                    power(ln3_rstd[:, :], ln3_var[:, :], 0, SUB).then_inc(sem["ln3_rstd_ready"], 1)
                if step == 16:
                    if isinstance(j, int) and j == 0:
                        pool.wait_ge(sem["zeroed_slots"], 16 * (SLOTS // (P * 16)))
                    pool.wait_ge(sem["slots_ready"], j + 1)
                    pool.wait_ge(sem["rows_ready"], 3 * j + 2)
                    pool.sem_inc(sem["passed"], 1)
                    for c in range(SUB):
                        for n in range(2):
                            g.indirect_dma_start(
                                slots_in, bass.IndirectOffsetOnAxis(ap=slot_scatter[:, 2 * c + n:2 * c + n + 1], axis=0),
                                x3_rows[:, n, c, :], None, bounds_check=SLOTS - 1, oob_is_err=False).then_inc(sem["scattered"], 16)

            pipeline(pool, (mix, wkv, ffn, gru))
            experts_pool(pool)
            last_pool(pool)


def pack_params(a):
    import numpy as np

    def put(rows, width):
        full = np.zeros((P, width), np.float32)
        full[:rows.shape[0]] = rows
        return full

    def column(x):
        return np.asarray(x).reshape(-1, P).T

    def row(x):
        return np.broadcast_to(np.asarray(x).reshape(1, -1), (P, np.asarray(x).size))

    eye = np.eye(P, dtype=np.float32)
    head = np.arange(P) // HS
    same = (head[:, None] == head[None, :]).astype(np.float32)
    before = (np.arange(P)[:, None] < np.arange(P)[None, :]).astype(np.float32)
    group_var = (head[:, None] == np.arange(HEADS)[None, :]).astype(np.float32) * (4.0 / HS)
    low_rows = -((np.arange(P) // E0) == 2).astype(np.float32)[:, None]
    spread = (np.arange(E0)[:, None] == (np.arange(2 * P) // INNER)[None, :]).astype(np.float32)
    lora_b = np.asarray(a["L0_attn_B_lora"])
    fields = {
        "ident": eye, "centre": (eye - 1.0 / P).astype(np.float32), "group_centre": (eye - same / HS).astype(np.float32),
        "upper": before, "ones": np.ones((P, P), np.float32), "mean_col": np.full((P, 2), 1.0 / P, np.float32),
        "group_var": group_var, "spread": put(np.concatenate([spread, spread]), 2 * P),
        "descend": row(np.tile(np.arange(E0, 0, -1), SUB).astype(np.float32)),
        "dest_base": (np.arange(P)[:, None] * (2 * SUB) + np.arange(2 * SUB)[None, :]).astype(np.float32),
        "slot_base": row(np.tile(np.arange(E1) * CAP, SUB).astype(np.float32)),
        "lora_a": a["L0_attn_A_lora"], "lora_b": lora_b[0:4].reshape(P, P), "lora_b4": put(lora_b[4], P),
        "td_a": a["L0_attn_td_A"], "td_b": put(np.asarray(a["L0_attn_td_B"]), P),
        "wk": np.asarray(a["L0_attn_Wk"]).T, "wv": np.asarray(a["L0_attn_Wv"]).T, "wr": np.asarray(a["L0_attn_Wr"]).T,
        "wg": np.asarray(a["L0_attn_Wg"]).T, "wo": a["L0_attn_Wo"],
        "fv": np.asarray(a["L0_ffn_Wv"]).T, "fv_raw": a["L0_ffn_Wv"],
        "f_router": np.concatenate([np.asarray(a["L0_ffn_Wg"]), np.asarray(a["L0_ffn_Wp"]).reshape(E0 * PROTO, P)]).T,
        "f_w1": np.asarray(a["L0_ffn_W1"]).reshape(2 * P, P).T,
        "f_w2": np.asarray(a["L0_ffn_W2"]).transpose(1, 0, 2).reshape(P, 2 * P), "f_b2": np.tile(np.asarray(a["L0_ffn_b2"]).T, (1, 3)), "low_rows": low_rows,
        "wz": np.asarray(a["L1_attn_W_z"]).T, "wh": np.asarray(a["L1_attn_W_h"]).T, "e_router": a["L1_ffn_Wr"],
        "miu_x": column(a["L0_attn_miu_x"]), "lam": column(a["L0_attn_lambda_"]), "td_miu": column(a["L0_attn_td_miu"]),
        "bonus": column(a["L0_attn_u"]), "gn_gamma": column(a["L0_attn_gn_gamma"]), "gn_beta": column(a["L0_attn_gn_beta"]),
        "f_bv": column(a["L0_ffn_bv"]), "f_b1": column(a["L0_ffn_b1"]), "b_z": column(a["L1_attn_b_z"]), "b_h": column(a["L1_attn_b_h"]),
        "f_bg": row(a["L0_ffn_bg"]), "f_gr": row(a["L0_ffn_g_r"]), "f_br": row(a["L0_ffn_b_r"]), "f_gc": row(a["L0_ffn_g_c"]),
        "f_bc": row(a["L0_ffn_b_c"]), "alpha": row(a["L0_ffn_alpha"]), "e_br": row(a["L1_ffn_br"]),
    }
    for name, width in FIELDS:
        assert np.asarray(fields[name]).shape == (P, width), name
    return np.ascontiguousarray(np.concatenate([np.asarray(fields[name]) for name, _ in FIELDS], axis=1))


def pack_experts(a):
    import numpy as np

    w1 = np.asarray(a["L1_ffn_W1"])
    w2 = np.asarray(a["L1_ffn_W2"]).reshape(E1, KT, P, P).transpose(0, 2, 1, 3).reshape(E1, P, HID)
    b1 = np.asarray(a["L1_ffn_b1"]).reshape(E1, KT, P).transpose(0, 2, 1)
    b2 = np.asarray(a["L1_ffn_b2"])[:, :, None]
    return np.ascontiguousarray(np.concatenate([w1, w2, b1, b2], axis=2))


def level_masks():
    import numpy as np

    src = (np.arange(P) % 64)[:, None]
    dst = np.arange(64)[None, :]
    found = [src == dst]
    for level in range(LEVELS):
        b = 1 << level
        found.append((src // (2 * b) == dst // (2 * b)) & (src % (2 * b) < b) & (dst % (2 * b) >= b))
    return np.ascontiguousarray(np.stack(found, axis=1).astype(np.uint32))


def kernel(**inputs):
    import numpy as np
    import concourse.bacc as bacc
    from concourse.bass_utils import run_bass_kernel_spmd as run

    nc = bacc.Bacc("TRN2", target_bir_lowering=False, num_devices=1)
    arrays = {
        "x_t": np.ascontiguousarray(np.asarray(inputs["L0_attn_x"]).transpose(0, 2, 1)),
        "params": pack_params(inputs),
        "masks": level_masks(),
        "experts": pack_experts(inputs),
    }
    args = [nc.dram_tensor(n, a.shape, mybir.dt.from_np(a.dtype), kind="ExternalInput").ap() for n, a in arrays.items()]
    args.append(nc.dram_tensor("out_0_dram", (B, T, P), F32, kind="ExternalOutput").ap())
    build_network(nc, *args)
    r = run(nc, [arrays], core_ids=[0])
    return r.results[0]["out_0_dram"]
```
